# Optimizing a Trainium2 kernel written in Bass

```python
import numpy as np
import jax
import jax.numpy as jnp

def _softmax(x, axis=-1):
    return jax.nn.softmax(x, axis=axis)

def _gelu(x):
    return jax.nn.gelu(x, approximate=True)

def _silu(x):
    return jax.nn.silu(x)

def _sigmoid(x):
    return jax.nn.sigmoid(x)

def _layernorm(x, axis=-1, eps=1e-05):
    m = jnp.mean(x, axis=axis, keepdims=True)
    v = jnp.var(x, axis=axis, keepdims=True)
    return (x - m) / jnp.sqrt(v + eps)

def _scatter_add(tgt, idx, src, axis=0):
    return tgt.at[idx].add(src)

def _segment_sum(src, seg, n):
    return jax.ops.segment_sum(src, seg, n)
kernel_name = 'mk_adj_ffn_d1_adj_r2_368e29'

def setup_inputs(seed: int=0):
    np.random.seed(seed)
    _w = jnp.asarray

    def _rec_inputs():
        import jax
        import jax.numpy as jnp
        _gk = jax.random.key(seed)
        x = -0.0002928 + 1 * jax.random.normal(jax.random.fold_in(_gk, 1), (2048, 256), jnp.float32)
        _a = jax.random.bernoulli(jax.random.fold_in(_gk, 2), 0.000976562, (2048, 2048))
        _a = jnp.logical_or(_a, jnp.swapaxes(_a, -1, -2))
        _a = jnp.logical_or(_a, jnp.eye(2048, dtype=bool))
        adj = _a.astype(jnp.int32)
        return (x, adj)
    x, adj = _rec_inputs()

    def _L0_gnn_setup():
        import jax, jax.numpy as jnp
        import numpy as np
        N, D_IN, D_OUT = (4096, 256, 256)
        key = jax.random.key(seed)
        ks = jax.random.split(key, 8)
        scale_in = 1.0 / np.sqrt(D_IN)
        scale_cat = 1.0 / np.sqrt(2 * D_OUT)
        return {'x': jax.random.normal(ks[0], (N, D_IN), dtype=jnp.float32), 'adj': jax.random.randint(ks[1], (N, N), 0, 2, dtype=jnp.int32), 'W_self': jax.random.uniform(ks[2], (D_IN, D_OUT), jnp.float32, -scale_in, scale_in), 'b_self': jax.random.uniform(ks[3], (D_OUT,), jnp.float32, -scale_in, scale_in), 'W_nb': jax.random.uniform(ks[4], (D_IN, D_OUT), jnp.float32, -scale_in, scale_in), 'b_nb': jax.random.uniform(ks[5], (D_OUT,), jnp.float32, -scale_in, scale_in), 'W_comb': jax.random.uniform(ks[6], (2 * D_OUT, D_OUT), jnp.float32, -scale_cat, scale_cat), 'b_comb': jax.random.uniform(ks[7], (D_OUT,), jnp.float32, -scale_cat, scale_cat)}
    _L0_gnn_all = _L0_gnn_setup()
    _L0_gnn_in = {k: v for k, v in _L0_gnn_all.items() if k in ('W_self', 'b_self', 'W_nb', 'b_nb', 'W_comb', 'b_comb')}
    del _L0_gnn_all

    def _L0_ffn_setup():
        import jax, jax.numpy as jnp
        import numpy as np
        B, S, H, I, E, K = (8, 2048, 256, 1024, 8, 2)
        key = jax.random.key(seed)
        ks = jax.random.split(key, 7)
        sH = 1.0 / np.sqrt(H)
        sI = 1.0 / np.sqrt(I)
        return {'x': jax.random.normal(ks[0], (B, S, H), dtype=jnp.float32), 'gate_w': jax.random.uniform(ks[1], (H, E), jnp.float32, -sH, sH), 'gate_b': jnp.zeros((E,), jnp.float32), 'w1': jax.random.uniform(ks[2], (E, H, I), jnp.float32, -sH, sH), 'b1': jax.random.uniform(ks[3], (E, I), jnp.float32, -sH, sH), 'w2': jax.random.uniform(ks[4], (E, I, H), jnp.float32, -sI, sI), 'b2': jax.random.uniform(ks[5], (E, H), jnp.float32, -sI, sI)}
    _L0_ffn_all = _L0_ffn_setup()
    _L0_ffn_in = {k: v for k, v in _L0_ffn_all.items() if k in ('gate_w', 'gate_b', 'w1', 'b1', 'w2', 'b2')}
    del _L0_ffn_all
    return {'x': x, 'adj': adj, 'L0_gnn_W_self': _L0_gnn_in['W_self'], 'L0_gnn_b_self': _L0_gnn_in['b_self'], 'L0_gnn_W_nb': _L0_gnn_in['W_nb'], 'L0_gnn_b_nb': _L0_gnn_in['b_nb'], 'L0_gnn_W_comb': _L0_gnn_in['W_comb'], 'L0_gnn_b_comb': _L0_gnn_in['b_comb'], 'L0_ffn_gate_w': _L0_ffn_in['gate_w'], 'L0_ffn_gate_b': _L0_ffn_in['gate_b'], 'L0_ffn_w1': _L0_ffn_in['w1'], 'L0_ffn_b1': _L0_ffn_in['b1'], 'L0_ffn_w2': _L0_ffn_in['w2'], 'L0_ffn_b2': _L0_ffn_in['b2']}

def reference(x, adj, L0_gnn_W_self, L0_gnn_b_self, L0_gnn_W_nb, L0_gnn_b_nb, L0_gnn_W_comb, L0_gnn_b_comb, L0_ffn_gate_w, L0_ffn_gate_b, L0_ffn_w1, L0_ffn_b1, L0_ffn_w2, L0_ffn_b2):
    import jax
    import jax.numpy as jnp

    def _L0_gnn_ref(x, adj, W_self, b_self, W_nb, b_nb, W_comb, b_comb):
        import jax, jax.numpy as jnp
        import numpy as np
        N, D_IN, D_OUT = (4096, 256, 256)
        mask = (adj > 0).astype(x.dtype)
        deg = jnp.sum(mask, axis=1, keepdims=True)
        agg = mask @ x / jnp.maximum(deg, 1.0)
        self_f = x @ W_self + b_self
        nb_f = agg @ W_nb + b_nb
        combined = jnp.concatenate([self_f, nb_f], axis=-1)
        out = combined @ W_comb + b_comb
        return jax.nn.relu(out)

    def _L0_ffn_ref(x, gate_w, gate_b, w1, b1, w2, b2):
        import jax, jax.numpy as jnp
        import numpy as np
        B, S, H, I, E, K = (8, 2048, 256, 1024, 8, 2)
        gate_probs = jax.nn.softmax(x @ gate_w + gate_b, axis=-1)
        top_v, top_i = jax.lax.top_k(gate_probs, K)
        top_w = jax.nn.softmax(top_v, axis=-1)
        out = jnp.zeros_like(x)
        for e in range(E):
            ce = jnp.sum(jnp.where(top_i == e, top_w, 0.0), axis=-1)
            h = jax.nn.relu(jnp.einsum('bsh,hi->bsi', x, w1[e]) + b1[e])
            ye = jnp.einsum('bsi,ih->bsh', h, w2[e]) + b2[e]
            out = out + ce[..., None] * ye
        return out
    x = x + _L0_gnn_ref(_layernorm(x, axis=-1), adj, L0_gnn_W_self, L0_gnn_b_self, L0_gnn_W_nb, L0_gnn_b_nb, L0_gnn_W_comb, L0_gnn_b_comb)
    x = x + _L0_ffn_ref(_layernorm(x, axis=-1)[None], L0_ffn_gate_w, L0_ffn_gate_b, L0_ffn_w1, L0_ffn_b1, L0_ffn_w2, L0_ffn_b2)[0]
    return x

_drawn_inputs = setup_inputs


def setup_inputs(seed=0):
    import zlib

    import numpy as np

    out = dict(_drawn_inputs(seed))
    spreads = {'L0_ffn_gate_b': (0.0, 0.1)}
    factors = {'L0_gnn_b_self': 3.321, 'L0_gnn_b_nb': 3.139, 'L0_ffn_b1': 5.527, 'L0_ffn_b2': 4.428}
    for name, (base, spread) in spreads.items():
        noise = np.random.default_rng([zlib.crc32(name.encode()), seed]).standard_normal(out[name].shape)
        drawn = base * np.exp(spread * noise) if base else spread * noise
        out[name] = jnp.asarray(drawn.astype(out[name].dtype))
    for name, factor in factors.items():
        out[name] = (out[name] * factor).astype(out[name].dtype)
    return out
```

```python
from contextlib import ExitStack

import concourse.bass as bass
from concourse import mybir

F32 = mybir.dt.float32
F16 = mybir.dt.float16
BF16 = mybir.dt.bfloat16
I32 = mybir.dt.int32
U32 = mybir.dt.uint32
ALU = mybir.AluOpType
ACT = mybir.ActivationFunctionType
AX = mybir.AxisListType.X
RADD = bass.bass_isa.ReduceOp.add
AT = bass.IndirectOffsetOnAxis

P = 128
EPS = 1e-5
TOP_EXP = 15


def wait(eng, sem, value):
    if isinstance(value, int) and value <= 0:
        return
    eng.wait_ge(sem, value)


def gnn_moe_kernel(nc, x, adj, w_self, b_self, w_nb, b_nb, w_comb, b_comb,
                   gate_w, gate_b, w1, b1, w2, b2, out):
    N, D = x.shape
    E, _, I = w1.shape
    KD = D // P
    KI = I // P
    NT = N // P
    HJ = NT // 2
    SLOT_TILES = (2 * N + E * (P - 1)) // P
    BLOCKS = N // P
    ROW = D + 2
    assert NT == 2 * E and BLOCKS * E == P and KD == 2

    hrows = nc.dram_tensor("hrows", [N, ROW], F32, kind="Internal").ap()
    idtab = nc.dram_tensor("idtab", [P, P], I32, kind="Internal").ap()
    idtab_flat = idtab.rearrange("b (s a) -> (b s) a", a=1)

    with ExitStack() as ctx:
        def sb(name, shape, dt):
            return ctx.enter_context(nc.sbuf_tensor(name, shape, dt))

        def psum(name, shape, dt):
            return ctx.enter_context(nc.psum_tensor(name, shape, dt))

        def sem(name):
            return ctx.enter_context(nc.semaphore(name))

        W1H = sb("W1H", [P, E, KD, I], F16)
        W1L = sb("W1L", [P, E, KD, I], F16)
        W2H = sb("W2H", [P, E, KI, D], F16)
        W2L = sb("W2L", [P, E, KI, D], F16)
        XH = sb("XH", [P, NT, D + 2], F16)
        XL = sb("XL", [P, NT, D], F16)
        adj_rows = sb("adj_rows", [P, 2, N], BF16)
        w_stage = sb("w_stage", [P, 2, KD * I], F32)
        maskT = sb("maskT", [P, 2, NT, P], F16)

        scr1 = W1L[:, E // 2:E].rearrange("p e k i -> p (e k i)").bitcast(F32)
        scr2 = W2L[:, E // 2:E].rearrange("p e k i -> p (e k i)").bitcast(F32)
        x0 = scr2.rearrange("p (t d) -> p t d", d=D)
        raw_self = scr1[:, 0:512].rearrange("p (k d) -> p k d", k=KD)
        raw_nb = scr1[:, 512:1024].rearrange("p (k d) -> p k d", k=KD)
        raw_comb = scr1[:, 1024:2048].rearrange("p (k d) -> p k d", k=2 * KD)
        selfT = scr1[:, 2048:2560].rearrange("p (k d) -> p k d", k=KD)
        nbT = scr1[:, 2560:3072].rearrange("p (k d) -> p k d", k=KD)
        bias_cols = scr1[:, 3072:3584].rearrange("p (k m) -> p k m", k=2 * KD)
        NB = E * KI + 2 * KD
        b_rows = scr1[0:NB, 3584:3712]
        b1sq = scr1[:, 3776:3840]

        ws_prod = sb("ws_prod", [P, KD, D], F32)
        wn_prod = sb("wn_prod", [P, KD, D], F32)
        bias = sb("bias", [P, D], F32)
        gw = sb("gw", [P, KD, E], F32)
        gb = sb("gb", [P, E], F32)
        bT = sb("bT", [P, NB], F32)
        b1T = bT[:, 0:E * KI].rearrange("p (e c) -> p e c", e=E)
        ident_f = sb("ident_f", [P, P], F32)
        ident_b = sb("ident_b", [P, P], BF16)
        ident_h = sb("ident_h", [P, P], F16)
        before = sb("before", [P, P], BF16)
        ones_b = sb("ones_b", [P, P], BF16)
        iota_e = sb("iota_e", [P, E], F32)
        expert_base = sb("expert_base", [P, E], F32)
        iota_p = sb("iota_p", [P, 1], F32)
        iota_f = sb("iota_f", [P, P], F32)
        slot_ids = sb("slot_ids", [P, NT * 2], I32)
        zero_ids = sb("zero_ids", [P, P], I32)
        minus_half = sb("minus_half", [P, NT], F32)

        ln_stat = sb("ln_stat", [P, NT, 6], F32)
        ln_mv = sb("ln_mv", [P, NT, 2], F32)
        ln_ve = sb("ln_ve", [P, NT], F32)
        ln_rs = sb("ln_rs", [P, NT], F32)
        x32 = sb("x32", [P, D], F32)
        aggn = sb("aggn", [P, D], F32)
        cT = sb("cT", [P, 4, P], F32)
        pre = sb("pre", [P, D], F32)
        x1 = sb("x1", [P, 2, D], F32)
        h32 = sb("h32", [P, D], F32)
        hT = sb("hT", [P, KD, P], F32)
        hrow = sb("hrow", [P, 2, ROW], F32)
        deg = sb("deg", [P, 2], F32)
        rdeg = sb("rdeg", [P, 2], F32)
        st2 = sb("st2", [P, 6], F32)
        mv2 = sb("mv2", [P, 2, 2], F32)
        ve2 = sb("ve2", [P, 2], F32)
        rs2 = sb("rs2", [P, 2], F32)
        lg = sb("lg", [P, E], F32)
        lmax = sb("lmax", [P, 1], F32)
        lshift = sb("lshift", [P, E], F32)
        pexp = sb("pexp", [P, E], F32)
        psum_e = sb("psum_e", [P, 1], F32)
        prec = sb("prec", [P, 1], F32)
        prob = sb("prob", [P, E], F32)
        top = sb("top", [P, 8], F32)
        top_i = sb("top_i", [P, 8], U32)
        top_f = sb("top_f", [P, 2], F32)
        vdiff = sb("vdiff", [P, 1], F32)
        ediff = sb("ediff", [P, 1], F32)
        eplus = sb("eplus", [P, 1], F32)
        gate0 = sb("gate0", [P, 1], F32)
        pick = sb("pick", [P, 2, E], F32)
        chosen = sb("chosen", [P, E], BF16)
        chosen_sum = sb("chosen_sum", [P, E], BF16)
        place = sb("place", [P, E], F32)
        pjunk = sb("pjunk", [P, 2, E], F32)
        dest = sb("dest", [P, 2], F32)
        dest_i = sb("dest_i", [P, 2, 2], I32)
        ssq = sb("ssq", [P, 2], F32)
        fro_now = sb("fro_now", [P, 2], F32)
        fro = sb("fro", [P, 2 * E], F32)
        half_exp = sb("half_exp", [P, 2 * E], I32)
        w_scale = sb("w_scale", [P, 2 * E], I32)
        w_inv = sb("w_inv", [P, 2 * E], I32)
        b1q = sb("b1q", [P, E], F32)
        b1fro = sb("b1fro", [P, E], F32)
        hq = sb("hq", [P, E], F32)
        h_half = sb("h_half", [P, E], I32)
        h_scale = sb("h_scale", [P, E], I32)
        h_inv = sb("h_inv", [P, E], I32)
        scaleA = sb("scaleA", [P, E], F32)
        biasA = sb("biasA", [P, E, KI], F32)
        scaleY = sb("scaleY", [P, E], F32)

        cnt = sb("cnt", [P, E], F32)
        cnt_i = sb("cnt_i", [P, E], I32)
        tiles_i = sb("tiles_i", [P, E], I32)
        ntile = sb("ntile", [P, E], F32)
        pfx = sb("pfx", [P, 3, E], F32)
        start_t = sb("start_t", [P, E], F32)
        past = sb("past", [P, E], F32)
        owns = sb("owns", [P, E], F32)
        local = sb("local", [P, E], F32)
        blk = sb("blk", [P, E], F32)
        left = sb("left", [P, E], F32)
        tjunk = sb("tjunk", [P, 3, E], F32)
        tcol = sb("tcol", [P, 3], F32)
        blk_i = sb("blk_i", [P, 1], I32)
        expert_blk = sb("expert_blk", [P, E], F32)
        ids = sb("ids", [P, P], I32)
        tok_i = sb("tok_i", [P, 2, P], I32)
        tok_f = sb("tok_f", [P, 3, P], F32)
        beyond = sb("beyond", [P, P], F32)
        tile_src = sb("tile_src", [P, SLOT_TILES], I32)
        tile_dst = sb("tile_dst", [P, SLOT_TILES], I32)
        ids_now = sb("ids_now", [P, 2, 2], I32)
        src_now = sb("src_now", [P, 2], I32)
        dst_now = sb("dst_now", [P, 2], I32)
        tile_choice = sb("tile_choice", [P, SLOT_TILES], F32)
        tile_expert = sb("tile_expert", [1, SLOT_TILES], I32)

        ws_flat = w_stage[:].rearrange("p u n -> p (u n)")
        act32 = ws_flat[:, 0:KI * P].rearrange("p (c s) -> p c s", c=KI)
        hid_h = ws_flat[:, 1024:2048].bitcast(F16).rearrange("p (b c s) -> p b c s", b=2, c=KI)
        hid_l = ws_flat[:, 2048:3072].bitcast(F16).rearrange("p (b c s) -> p b c s", b=2, c=KI)
        b2_all = adj_rows[:].rearrange("p u n -> p (u n)").bitcast(F32).rearrange("p (e d) -> p e d", e=E)
        XL_flat = XL[:].rearrange("p t d -> p (t d)")
        mt_flat = maskT[:].rearrange("p u j s -> p (u j s)")
        xg = mt_flat[:, 0:4 * ROW].bitcast(F32).rearrange("p (b d) -> p b d", b=2)
        xgT = mt_flat[:, 2080:3104].rearrange("p (b j s) -> p b j s", b=2, j=4)
        yg = XL_flat[:, 0:1024].bitcast(F32).rearrange("p (b d) -> p b d", b=2)
        y32 = XL_flat[:, 1024:1536].bitcast(F32)
        gate = sb("gate", [P, SLOT_TILES], F32)

        bank = [psum(f"bank{i}", [P, 512], F32) for i in range(8)]
        mask_ps = [bank[i][:].bitcast(BF16).rearrange("p (j s) -> p j s", s=P) for i in range(2)]
        agg_ps = [bank[2], bank[3]]
        trx_ps = bank[4][:].rearrange("p (k s) -> p k s", s=P)
        pre_ps = bank[5][:, 0:D]
        hT_ps = bank[6][:, 0:D].rearrange("p (k s) -> p k s", s=P)
        lg_ps = bank[7][:, 0:E]
        rank_ps = bank[7][:, 16:16 + E]
        cnt_ps = bank[7][:, 32:32 + E]

        s_xin = [sem(f"s_xin{g}") for g in range(4)]
        s_wself = sem("s_wself")
        s_wcomb = sem("s_wcomb")
        s_small = sem("s_small")
        s_const = sem("s_const")
        s_set = sem("s_set")
        s_rstd = sem("s_rstd")
        s_xn = sem("s_xn")
        s_xh = sem("s_xh")
        s_xl = sem("s_xl")
        s_setT = sem("s_setT")
        s_setTc = sem("s_setTc")
        s_setP = sem("s_setP")
        s_setPc = sem("s_setPc")
        s_bcols = sem("s_bcols")
        s_bias = sem("s_bias")
        s_b1T = sem("s_b1T")
        s_b1q = sem("s_b1q")
        s_b1f = sem("s_b1f")
        s_gps = sem("s_gps")
        s_idz = sem("s_idz")

        s_adj = [sem(f"s_adj{u}") for u in range(2)]
        s_w = [sem(f"s_w{u}") for u in range(2)]
        s_x = [sem(f"s_xrow{u}") for u in range(2)]
        s_x1st = [sem(f"s_x1st{u}") for u in range(2)]
        s_hst = [sem(f"s_hst{u}") for u in range(2)]
        s_idst = [sem(f"s_idst{u}") for u in range(2)]
        s_tr = [sem("s_trA"), sem("s_trB")]
        s_mask = [sem("s_maskA"), sem("s_maskB")]
        s_agg = sem("s_agg")
        s_deg = sem("s_deg")
        s_rdeg = sem("s_rdeg")
        s_aggn = sem("s_aggn")
        s_x32 = sem("s_x32")
        s_ct = sem("s_ct")
        s_ctc = sem("s_ctc")
        s_pre = sem("s_pre")
        s_prec = sem("s_prec")
        s_x1 = sem("s_x1")
        s_ln = sem("s_ln")
        s_ve = sem("s_ve")
        s_rs = sem("s_rs")
        s_h = sem("s_h")
        s_ht = sem("s_ht")
        s_htc = sem("s_htc")
        s_lg = sem("s_lg")
        s_gate = sem("s_gate")
        s_shift = sem("s_shift")
        s_pexp = sem("s_pexp")
        s_vdiff = sem("s_vdiff")
        s_ediff = sem("s_ediff")
        s_meta = sem("s_meta")
        s_chosen = sem("s_chosen")
        s_rank = sem("s_rank")
        s_dest = sem("s_dest")
        s_hlo = sem("s_hlo")
        s_hhi = sem("s_hhi")
        s_sq = sem("s_sq")
        s_fro = sem("s_fro")
        s_scl = sem("s_scl")
        s_frc = sem("s_frc")
        s_scale = sem("s_scale")
        s_whi = sem("s_whi")
        s_wlo = sem("s_wlo")

        s_cnt = sem("s_cnt")
        s_tab = sem("s_tab")
        s_blk = sem("s_blk")
        s_ids = sem("s_ids")
        s_tokf = sem("s_tokf")
        s_tabT = sem("s_tabT")
        s_table = sem("s_table")
        s_prm = sem("s_prm")
        s_param = sem("s_param")
        s_b2 = sem("s_b2")

        s_xg = [sem(f"s_xg{u}") for u in range(2)]
        s_src = sem("s_src")
        s_idn = sem("s_idn")
        s_dst = sem("s_dst")
        s_xgT = sem("s_xgT")
        s_xgc = sem("s_xgc")
        s_wsel = sem("s_wsel")
        s_gt = sem("s_gt")
        s_mm1 = [sem("s_mm1A"), sem("s_mm1B")]
        s_act = [sem("s_actA"), sem("s_actB")]
        s_hidh = [sem("s_hidhA"), sem("s_hidhB")]
        s_hidl = [sem("s_hidlA"), sem("s_hidlB")]
        s_mm2 = sem("s_mm2")
        s_y32 = sem("s_y32")
        s_yg = sem("s_yg")
        s_add = sem("s_add")

        x_t = x.rearrange("(t p) d -> t p d", p=P)
        out_t = out.rearrange("(t p) d -> t p d", p=P)
        adj_t = adj.rearrange("(t p) j -> t p j", p=P)
        hrows_t = hrows.rearrange("(t p) d -> t p d", p=P)
        w1_t = w1.rearrange("e (k p) i -> e p k i", p=P)
        w2_t = w2.rearrange("e (c p) d -> e p c d", p=P)

        def stage_w(u):
            return w_stage[:, u].rearrange("p (k i) -> p k i", k=KD if u == 0 else KI)

        def wsplit(u, e):
            hi, lo = (W1H, W1L) if u == 0 else (W2H, W2L)
            return hi[:, e], lo[:, e]

        LAST = NT + 1

        def graph_steps(eng, step):
            for s in range(4):
                step(s, s % 2, s // 2)
            with eng.Fori(0, NT // 2 - 3) as q:
                for u in range(2):
                    step(q * 2 + (4 + u), u, q + 2)
            for s in range(NT - 2, NT + 2):
                step(s, s % 2, s // 2)

        def is_step(s, lo, hi):
            return not isinstance(s, int) or lo <= s <= hi

        def slot_steps(eng, step):
            step(0, 0, 0)
            step(1, 1, 0)
            with eng.Fori(0, SLOT_TILES // 2 - 1) as q:
                for u in range(2):
                    step(q * 2 + (2 + u), u, q + 1)
            step(SLOT_TILES - 1, 0, SLOT_TILES // 2)

        assert SLOT_TILES % 2 == 1

        block = ctx.enter_context(nc.Block())

        @block.sync
        def _(sp):
            for g in range(4):
                sp.dma_start(x0[:, 4 * g:4 * g + 4], x_t[4 * g:4 * g + 4].rearrange("t p d -> p t d")).then_inc(s_xin[g], 16)
            sp.dma_start(raw_self, w_self.rearrange("(k p) d -> p k d", p=P)).then_inc(s_wself, 16)
            sp.dma_start(raw_nb, w_nb.rearrange("(k p) d -> p k d", p=P)).then_inc(s_wself, 16)
            sp.dma_start(raw_comb, w_comb.rearrange("(k p) d -> p k d", p=P)).then_inc(s_wcomb, 16)
            sp.dma_start(b_rows[E * KI:E * KI + KD, :], b_self.rearrange("(k p) -> k p", p=P)).then_inc(s_small, 16)
            sp.dma_start(b_rows[E * KI + KD:NB, :], b_nb.rearrange("(k p) -> k p", p=P)).then_inc(s_small, 16)
            sp.dma_start(bias[:], b_comb.partition_broadcast(P)).then_inc(s_small, 16)
            sp.dma_start(gw[:], gate_w.rearrange("(k p) e -> p k e", p=P)).then_inc(s_small, 16)
            sp.dma_start(gb[:], gate_b.partition_broadcast(P)).then_inc(s_small, 16)
            sp.dma_start(b_rows[0:E * KI, :], b1.rearrange("e (c p) -> (e c) p", p=P)).then_inc(s_small, 16)

            def load_w(i, u, k):
                src = w1_t if u == 0 else w2_t
                e = k
                sp.dma_start(stage_w(u), src[bass.ds(e, 1)].rearrange("a p k i -> p (a k) i")).then_inc(s_w[u], 16)

            load_w(0, 0, 0)
            load_w(1, 1, 0)

            def step(s, u, k):
                if is_step(s, 0, NT - 1):
                    wait(sp, s_h, s - 1)
                    wait(sp, s_x1st[u], 16 * k)
                    sp.dma_start(x1[:, u], x_t[bass.ds(s, 1)].rearrange("t p d -> p (t d)")).then_inc(s_x[u], 16)
                if is_step(s, 1, NT - 2):
                    wait(sp, s_wlo, s)
                    load_w(s + 1, 1 - u, k + u)
                if is_step(s, 1, NT):
                    wait(sp, s_x1, s)
                    sp.dma_start(out_t[bass.ds(s - 1, 1)].rearrange("t p d -> p (t d)"), x1[:, 1 - u]).then_inc(s_x1st[1 - u], 16)
                if is_step(s, 2, LAST):
                    wait(sp, s_hlo, s - 1)
                    wait(sp, s_meta, s - 1)
                    sp.dma_start(hrows_t[bass.ds(s - 2, 1)].rearrange("t p d -> p (t d)"), hrow[:, u]).then_inc(s_hst[u], 16)

            graph_steps(sp, step)
            sp.wait_ge(s_tr[1], NT)
            sp.dma_start(b2_all, b2.rearrange("e d -> (e d)").partition_broadcast(P).rearrange("p (e d) -> p e d", e=E)).then_inc(s_b2, 16)

        @block.gpsimd
        def _(pool):
            for t in (ident_f, ident_b, ident_h):
                pool.memset(t[:], 0.0).then_inc(s_gps, 1)
            pool.memset(before[:], 1.0).then_inc(s_gps, 1)
            pool.memset(zero_ids[:], 0).then_inc(s_gps, 1)
            pool.wait_ge(s_gps, 5)
            pool.dma_start(idtab, zero_ids[:]).then_inc(s_idz, 16)

            def load_adj(s, u):
                pool.dma_start(adj_rows[:, u], adj_t[bass.ds(s, 1)].rearrange("t p j -> p (t j)")).then_inc(s_adj[u], 16)

            load_adj(0, 0)
            load_adj(1, 1)
            for t in (ident_f, ident_b, ident_h):
                pool.affine_select(out=t[:], in_=t[:], compare_op=ALU.not_equal, fill=1.0, base=0,
                                   pattern=[[-1, P]], channel_multiplier=1).then_inc(s_const, 1)
            pool.affine_select(out=before[:], in_=before[:], compare_op=ALU.is_gt, fill=0.0, base=0,
                               pattern=[[1, P]], channel_multiplier=-1).then_inc(s_const, 1)
            pool.memset(ones_b[:], 1.0).then_inc(s_const, 1)
            pool.memset(XH[:, :, D:D + 2], 1.0).then_inc(s_const, 1)
            pool.memset(chosen_sum[:], 0.0).then_inc(s_const, 1)
            pool.memset(minus_half[:], -0.5).then_inc(s_const, 1)
            pool.iota(iota_e[:], pattern=[[1, E]], base=0, channel_multiplier=0, allow_small_or_imprecise_dtypes=True).then_inc(s_const, 1)
            pool.iota(expert_base[:], pattern=[[N, E]], base=0, channel_multiplier=0, allow_small_or_imprecise_dtypes=True).then_inc(s_const, 1)
            pool.iota(expert_blk[:], pattern=[[BLOCKS, E]], base=0, channel_multiplier=0, allow_small_or_imprecise_dtypes=True).then_inc(s_const, 1)
            pool.iota(iota_p[:], pattern=[[0, 1]], base=0, channel_multiplier=1, allow_small_or_imprecise_dtypes=True).then_inc(s_const, 1)
            pool.iota(iota_f[:], pattern=[[1, P]], base=0, channel_multiplier=0, allow_small_or_imprecise_dtypes=True).then_inc(s_const, 1)
            pool.iota(slot_ids[:].rearrange("p (t c) -> p t c", c=2), pattern=[[2 * P, NT], [1, 2]], base=0, channel_multiplier=2).then_inc(s_const, 1)
            pool.wait_ge(s_const, 14)
            pool.wait_ge(s_set, NT + NT + 1)
            pool.tensor_tensor(ln_rs[:], ln_ve[:], minus_half[:], ALU.pow).then_inc(s_rstd, 1)
            pool.wait_ge(s_b1q, 2)
            pool.partition_all_reduce(b1fro[:], b1q[:], P, RADD).then_inc(s_b1f, 1)
            pool.wait_ge(s_xl, 4)
            pool.wait_ge(s_xh, 4)
            pool.wait_ge(s_idz, 16)

            def step(s, u, k):
                if is_step(s, 2, LAST):
                    wait(pool, s_hst[u], 16 * (k - 1))
                    pool.nop(nofuse=True)
                    wait(pool, s_h, s - 1)
                    pool.nop(nofuse=True)
                    halves = hrow[:, u, 0:D].bitcast(F16)
                    pool.tensor_copy(halves[:, 0:D], h32[:]).then_inc(s_hhi, 1)
                    wait(pool, s_hhi, s - 1)
                    pool.nop(nofuse=True)
                    pool.tensor_tensor(halves[:, D:2 * D], h32[:], halves[:, 0:D], ALU.subtract).then_inc(s_hlo, 1)
                if is_step(s, 0, NT - 1):
                    wait(pool, s_ct, s)
                    pool.nop(nofuse=True)
                    src_h = XH[:, bass.ds(s, 1), 0:D].rearrange("p a d -> p (a d)")
                    src_l = XL[:, bass.ds(s, 1), :].rearrange("p a d -> p (a d)")
                    pool.tensor_tensor(x32[:], src_h, src_l, ALU.add).then_inc(s_x32, 1)
                if is_step(s, 0, NT - 3):
                    wait(pool, s_tr[1], s + 1)
                    pool.nop(nofuse=True)
                    load_adj(s + 2, u)
                if is_step(s, 0, NT - 1):
                    wait(pool, s_sq, s + 1)
                    pool.nop(nofuse=True)
                    pool.partition_all_reduce(fro_now[:, u:u + 1], ssq[:, u:u + 1], P, RADD).then_inc(s_fro, 1)
                if is_step(s, 1, NT):
                    wait(pool, s_ve, s)
                    pool.nop(nofuse=True)
                    pool.tensor_tensor(rs2[:, 1 - u:2 - u], ve2[:, 1 - u:2 - u], minus_half[:, 0:1], ALU.pow).then_inc(s_rs, 1)
                if is_step(s, 2, LAST):
                    wait(pool, s_dest, s - 1)
                    pool.nop(nofuse=True)
                    pool.tensor_copy(ids_now[:, u], slot_ids[:, bass.ds((s - 2) * 2, 2)]).then_inc(s_idn, 1)
                    wait(pool, s_idn, s - 1)
                    pool.nop(nofuse=True)
                    for c in range(2):
                        pool.indirect_dma_start(out=idtab_flat, out_offset=AT(ap=dest_i[:, u, c:c + 1], axis=0),
                                                in_=ids_now[:, u, c:c + 1], in_offset=None).then_inc(s_idst[u], 16)

            graph_steps(pool, step)

            for u in range(2):
                pool.wait_ge(s_idst[u], 32 * (NT // 2))
            pool.wait_ge(s_blk, 1)
            pool.indirect_dma_start(out=ids[0:SLOT_TILES, :], out_offset=None, in_=idtab,
                                    in_offset=AT(ap=blk_i[0:SLOT_TILES, 0:1], axis=0)).then_inc(s_ids, 16)
            for u in range(2):
                pool.wait_ge(s_hst[u], 16 * (NT // 2))
                pool.wait_ge(s_x1st[u], 16 * (NT // 2))
            pool.wait_ge(s_table, 1)

            def gather(t, u):
                pool.tensor_copy(src_now[:, u:u + 1], tile_src[:, bass.ds(t, 1)]).then_inc(s_src, 1)
                wait(pool, s_src, t + 1)
                pool.nop(nofuse=True)
                pool.indirect_dma_start(out=xg[:, u], out_offset=None, in_=hrows,
                                        in_offset=AT(ap=src_now[:, u:u + 1], axis=0)).then_inc(s_xg[u], 16)

            gather(0, 0)
            gather(1, 1)

            def step(t, u, k):
                if is_step(t, 0, SLOT_TILES - 3):
                    wait(pool, s_wsel, t + 1)
                    pool.nop(nofuse=True)
                    wait(pool, s_xgT, t + 1)
                    pool.nop(nofuse=True)
                    gather(t + 2, u)
                pool.tensor_copy(dst_now[:, u:u + 1], tile_dst[:, bass.ds(t, 1)]).then_inc(s_dst, 1)
                wait(pool, s_dst, t + 1)
                pool.nop(nofuse=True)
                wait(pool, s_yg, t + 1)
                pool.nop(nofuse=True)
                wait(pool, s_add, 16 * t)
                pool.nop(nofuse=True)
                pool.indirect_dma_start(out=out, out_offset=AT(ap=dst_now[:, u:u + 1], axis=0),
                                        in_=yg[:, u], in_offset=None, bounds_check=N - 1, oob_is_err=False,
                                        compute_op=ALU.add).then_inc(s_add, 16)

            step(0, 0, 0)
            step(1, 1, 0)
            with pool.Fori(0, SLOT_TILES // 2 - 2) as q:
                for u in range(2):
                    step(q * 2 + (2 + u), u, q + 1)
            for t in range(SLOT_TILES - 3, SLOT_TILES):
                step(t, t % 2, t // 2)
            pool.wait_ge(s_add, 16 * SLOT_TILES)

        @block.scalar
        def _(act):
            act.wait_ge(s_const, 6)
            for i, (src, dst) in enumerate(((bank[2], selfT), (bank[3], nbT))):
                act.wait_ge(s_setT, i + 1)
                act.activation(dst, src[:].rearrange("p (k d) -> p k d", k=KD), ACT.Copy).then_inc(s_setTc, 1)
            for i, (src, dst) in enumerate(((bank[4], ws_prod), (bank[5], wn_prod))):
                act.wait_ge(s_setP, i + 1)
                act.activation(dst[:], src[:].rearrange("p (k d) -> p k d", k=KD), ACT.Copy).then_inc(s_setPc, 1)
            for g in range(4):
                act.wait_ge(s_xn, g + 1)
                act.activation(XH[:, 4 * g:4 * g + 4, 0:D], x0[:, 4 * g:4 * g + 4], ACT.Copy).then_inc(s_xh, 1)

            def step(s, u, k):
                if is_step(s, 1, NT):
                    wait(act, s_rdeg, s)
                    wait(act, s_ct, s - 1)
                    act.activation(aggn[:], agg_ps[1 - u][:, 0:D], ACT.Copy, scale=rdeg[:, 1 - u:2 - u]).then_inc(s_aggn, 1)
                    wait(act, s_ct, s)
                    wait(act, s_pre, s - 1)
                    act.activation(cT[:], trx_ps, ACT.Copy).then_inc(s_ctc, 1)
                if is_step(s, 2, LAST):
                    wait(act, s_ht, s - 1)
                    wait(act, s_lg, s - 2)
                    act.activation(hT[:], hT_ps, ACT.Copy).then_inc(s_htc, 1)
                if is_step(s, 0, NT - 1):
                    hi, _ = wsplit(u, bass.ds(k, 1))
                    hi = hi.rearrange("p a k i -> p (a k i)")
                    wait(act, s_w[u], 16 * (k + 1))
                    wait(act, s_fro, s - 1)
                    act.activation(hi, w_stage[:, u], ACT.Square, accum_out=ssq[:, u:u + 1]).then_inc(s_sq, 1)
                if is_step(s, 2, LAST):
                    wait(act, s_shift, s - 1)
                    act.activation(pexp[:], lshift[:], ACT.Exp, accum_out=psum_e[:]).then_inc(s_pexp, 1)
                    wait(act, s_vdiff, s - 1)
                    act.activation(ediff[:], vdiff[:], ACT.Exp).then_inc(s_ediff, 1)
                if is_step(s, 0, NT - 1):
                    wait(act, s_scale, s + 1)
                    act.activation(hi, w_stage[:, u], ACT.Copy,
                                   scale=w_scale[:, bass.ds(s, 1)].bitcast(F32)).then_inc(s_whi, 1)

            graph_steps(act, step)

            act.wait_ge(s_param, 1)
            act.wait_ge(s_wlo, NT)
            act.wait_ge(s_table, 1)

            def step(t, u, k):
                e = act.value_load(tile_expert[0:1, bass.ds(t, 1)], min_val=0, max_val=E - 1)
                for half in range(2):
                    wait(act, s_mm1[half], t + 1)
                    wait(act, s_hidl[half], t)
                    for c in range(4 * half, 4 * half + 4):
                        src = bank[1 + 2 * u + half][:, (c % 4) * P:(c % 4 + 1) * P]
                        ins = act.activation(act32[:, c], src, ACT.Relu, scale=scaleA[:, bass.ds(e, 1)],
                                             bias=biasA[:, bass.ds(e, 1), c:c + 1].rearrange("p a c -> p (a c)"))
                    ins.then_inc(s_act[half], 1)

            slot_steps(act, step)

        @block.vector
        def _(dve):
            n = 0
            for g in range(4):
                dve.wait_ge(s_xin[g], 16)
                for t in range(4 * g, 4 * g + 4):
                    dve.bn_stats(ln_stat[:, t], x0[:, t]).then_inc(s_set, 1)
                    n += 1
            dve.wait_ge(s_set, n)
            for t in range(NT):
                dve.bn_aggr(ln_mv[:, t], ln_stat[:, t]).then_inc(s_set, 1)
                n += 1
            dve.wait_ge(s_set, n)
            dve.tensor_scalar(ln_ve[:], ln_mv[:, :, 1], EPS, None, ALU.add).then_inc(s_set, 1)
            n += 1
            dve.wait_ge(s_b1T, 1)
            dve.tensor_copy(bT[:], bank[7][:, 0:NB]).then_inc(s_b1q, 1)
            dve.wait_ge(s_b1q, 1)
            dve.wait_ge(s_const, 6)
            for i in range(2 * KD):
                dve.tensor_scalar(bias_cols[:, i], ones_b[:], bT[:, E * KI + i:E * KI + i + 1], None, ALU.mult).then_inc(s_bcols, 1)
            dve.wait_ge(s_rstd, 1)
            for g in range(4):
                for t in range(4 * g, 4 * g + 4):
                    ins = dve.tensor_scalar(x0[:, t], x0[:, t], ln_mv[:, t, 0:1], ln_rs[:, t:t + 1], ALU.subtract, ALU.mult)
                    if t % 4 < 3:
                        ins.then_inc(s_set, 1)
                        n += 1
                ins.then_inc(s_xn, 1)
                dve.wait_ge(s_set, n)
                dve.wait_ge(s_xn, g + 1)
                dve.wait_ge(s_xh, g + 1)
                dve.tensor_tensor(XL[:, 4 * g:4 * g + 4], x0[:, 4 * g:4 * g + 4], XH[:, 4 * g:4 * g + 4, 0:D], ALU.subtract).then_inc(s_xl, 1)
            dve.wait_ge(s_setP, 3)
            dve.tensor_tensor(bias[:], bank[6][:, 0:D], bias[:], ALU.add).then_inc(s_bias, 1)
            dve.tensor_tensor(b1sq, bT[:, 0:E * KI], bT[:, 0:E * KI], ALU.mult).then_inc(s_set, 1)
            n += 1
            dve.wait_ge(s_set, n)
            dve.tensor_reduce(b1q[:], b1sq.rearrange("p (e c) -> p e c", e=E), AX, ALU.add).then_inc(s_b1q, 1)
            dve.wait_ge(s_bias, 1)

            GATE = 15
            LN = 2

            def step(s, u, k):
                o = 1 - u
                if is_step(s, 1, NT):
                    wait(dve, s_agg, s)
                    dve.tensor_scalar(deg[:, o:o + 1], agg_ps[o][:, D:D + 1], 1.0, None, ALU.max).then_inc(s_deg, 1)
                    wait(dve, s_deg, s)
                    dve.reciprocal(rdeg[:, o:o + 1], deg[:, o:o + 1]).then_inc(s_rdeg, 1)
                if is_step(s, 2, LAST):
                    wait(dve, s_rs, s - 1)
                    wait(dve, s_ht, s - 2)
                    wait(dve, s_hlo, s - 2)
                    dve.tensor_scalar(h32[:], x1[:, u], mv2[:, u, 0:1], rs2[:, u:u + 1], ALU.subtract, ALU.mult).then_inc(s_h, 1)
                if is_step(s, 0, NT - 1):
                    for half in range(2):
                        wait(dve, s_tr[half], s + 1)
                        wait(dve, s_agg, s - 1)
                        dve.tensor_scalar(maskT[:, u, HJ * half:HJ * (half + 1)], mask_ps[half], 0.0, None,
                                          ALU.is_gt).then_inc(s_mask[half], 1)
                    col = bass.ds(s, 1)
                    wait(dve, s_fro, s + 1)
                    dve.tensor_copy(fro[:, col], fro_now[:, u:u + 1]).then_inc(s_frc, 1)
                    dve.tensor_scalar(half_exp[:, col], fro_now[:, u:u + 1].bitcast(I32), 24, None, ALU.logical_shift_right).then_inc(s_scl, 1)
                    wait(dve, s_scl, s + 1)
                    dve.tensor_scalar(w_scale[:, col], half_exp[:, col], -float(2 ** 23), float((189 + TOP_EXP) * 2 ** 23),
                                      ALU.mult, ALU.add).then_inc(s_scale, 1)
                if is_step(s, 1, NT):
                    hi, lo = wsplit(o, bass.ds(k if u else k - 1, 1))
                    wait(dve, s_whi, s)
                    dve.scalar_tensor_tensor(out=lo.rearrange("p a k i -> p (a k i)"), in0=w_stage[:, o],
                                             scalar=w_scale[:, bass.ds(s - 1, 1)].bitcast(F32),
                                             in1=hi.rearrange("p a k i -> p (a k i)"),
                                             op0=ALU.mult, op1=ALU.subtract).then_inc(s_wlo, 1)
                if is_step(s, 2, LAST):
                    r = s - 2
                    base, i = r * GATE, 0
                    wait(dve, s_lg, r + 1)
                    dve.tensor_tensor(lg[:], lg_ps, gb[:], ALU.add).then_inc(s_gate, 1)
                    wait(dve, s_gate, base + 1)
                    dve.tensor_reduce(lmax[:], lg[:], AX, ALU.max).then_inc(s_gate, 1)
                    wait(dve, s_gate, base + 2)
                    dve.tensor_scalar(lshift[:], lg[:], lmax[:], None, ALU.subtract).then_inc(s_shift, 1)
                    wait(dve, s_pexp, r + 1)
                    dve.reciprocal(prec[:], psum_e[:]).then_inc(s_gate, 1)
                    wait(dve, s_gate, base + 3)
                    dve.tensor_scalar(prob[:], pexp[:], prec[:], None, ALU.mult).then_inc(s_gate, 1)
                    wait(dve, s_gate, base + 4)
                    dve.nop(nofuse=True)
                    dve.max(top[:], prob[:]).then_inc(s_gate, 1)
                    wait(dve, s_gate, base + 5)
                    dve.tensor_tensor(vdiff[:], top[:, 1:2], top[:, 0:1], ALU.subtract).then_inc(s_vdiff, 1)
                    dve.max_index(top_i[:], top[:], prob[:]).then_inc(s_gate, 1)
                    wait(dve, s_gate, base + 6)
                    dve.tensor_copy(top_f[:], top_i[:, 0:2]).then_inc(s_gate, 1)
                    wait(dve, s_gate, base + 7)
                    for c in range(2):
                        dve.tensor_scalar(pick[:, c], iota_e[:], top_f[:, c:c + 1], None, ALU.is_equal).then_inc(s_gate, 1)
                    wait(dve, s_gate, base + 9)
                    wait(dve, s_rank, r)
                    dve.tensor_tensor(chosen[:], pick[:, 0], pick[:, 1], ALU.add).then_inc(s_chosen, 1)
                    wait(dve, s_ediff, r + 1)
                    dve.tensor_scalar(eplus[:], ediff[:], 1.0, None, ALU.add).then_inc(s_gate, 1)
                    wait(dve, s_gate, base + 10)
                    dve.reciprocal(gate0[:], eplus[:]).then_inc(s_gate, 1)
                    wait(dve, s_gate, base + 11)
                    wait(dve, s_hst[u], 16 * (k - 1))
                    meta = hrow[:, u, D:ROW]
                    dve.tensor_copy(meta[:, 0:1], gate0[:]).then_inc(s_gate, 1)
                    dve.scalar_tensor_tensor(out=meta[:, 1:2], in0=ediff[:], scalar=-1.0, in1=gate0[:],
                                             op0=ALU.add, op1=ALU.mult).then_inc(s_meta, 1)
                if is_step(s, 1, NT):
                    c, base = s - 1, (s - 1) * LN
                    wait(dve, s_pre, c + 1)
                    dve.tensor_tensor(pre[:], pre_ps, bias[:], ALU.add).then_inc(s_prec, 1)
                    wait(dve, s_prec, c + 1)
                    wait(dve, s_x[o], 16 * (k + u))
                    dve.scalar_tensor_tensor(out=x1[:, o], in0=pre[:], scalar=0.0, in1=x1[:, o],
                                             op0=ALU.max, op1=ALU.add).then_inc(s_x1, 1)
                    wait(dve, s_x1, c + 1)
                    dve.bn_stats(st2[:], x1[:, o]).then_inc(s_ln, 1)
                    wait(dve, s_ln, base + 1)
                    dve.nop(nofuse=True)
                    dve.bn_aggr(mv2[:, o], st2[:]).then_inc(s_ln, 1)
                    wait(dve, s_ln, base + 2)
                    dve.tensor_scalar(ve2[:, o:o + 1], mv2[:, o, 1:2], EPS, None, ALU.add).then_inc(s_ve, 1)
                if is_step(s, 2, LAST):
                    r, base = s - 2, (s - 2) * GATE
                    wait(dve, s_rank, r + 1)
                    dve.tensor_tensor(place[:], rank_ps, expert_base[:], ALU.add).then_inc(s_gate, 1)
                    dve.tensor_tensor(chosen_sum[:], chosen_sum[:], chosen[:], ALU.add).then_inc(s_gate, 1)
                    wait(dve, s_gate, base + 13)
                    for c in range(2):
                        ins = dve.tensor_tensor_reduce(pjunk[:, c], place[:], pick[:, c], 1.0, 0.0, ALU.mult, ALU.add, dest[:, c:c + 1])
                    ins.then_inc(s_gate, 1)
                    wait(dve, s_gate, base + 15)
                    wait(dve, s_idst[u], 32 * (k - 1))
                    dve.tensor_copy(dest_i[:, u], dest[:]).then_inc(s_dest, 1)

            graph_steps(dve, step)

            dve.wait_ge(s_cnt, 1)
            n = 0

            def link(ins):
                nonlocal n
                ins.then_inc(s_tab, 1)
                n += 1
                dve.wait_ge(s_tab, n)

            link(dve.tensor_copy(cnt[:], cnt_ps))
            link(dve.tensor_scalar(cnt_i[:], cnt[:], float(P - 1), None, ALU.add))
            link(dve.tensor_scalar(tiles_i[:], cnt_i[:], 7, None, ALU.logical_shift_right))
            link(dve.tensor_copy(ntile[:], tiles_i[:]))
            src = ntile[:]
            for i, d in enumerate((1, 2, 4)):
                link(dve.tensor_copy(pfx[:, i, 0:d], src[:, 0:d]))
                link(dve.tensor_tensor(pfx[:, i, d:E], src[:, d:E], src[:, 0:E - d], ALU.add))
                src = pfx[:, i]
            link(dve.tensor_tensor(start_t[:], src, ntile[:], ALU.subtract))
            link(dve.tensor_scalar(past[:], src, iota_p[:], None, ALU.is_le))
            link(dve.scalar_tensor_tensor(out=owns[:], in0=start_t[:], scalar=iota_p[:], in1=past[:], op0=ALU.is_le, op1=ALU.subtract))
            link(dve.tensor_scalar(local[:], start_t[:], iota_p[:], -1.0, ALU.subtract, ALU.mult))
            link(dve.tensor_tensor(blk[:], local[:], expert_blk[:], ALU.add))
            link(dve.scalar_tensor_tensor(out=left[:], in0=local[:], scalar=-float(P), in1=cnt[:], op0=ALU.mult, op1=ALU.add))
            for i, t in enumerate((blk, left, iota_e)):
                link(dve.tensor_tensor_reduce(tjunk[:, i], t[:], owns[:], 1.0, 0.0, ALU.mult, ALU.add, tcol[:, i:i + 1]))
            dve.tensor_copy(blk_i[:], tcol[:, 0:1]).then_inc(s_blk, 1)

            dve.wait_ge(s_b1f, 1)
            m = 0

            def plink(ins):
                nonlocal m
                ins.then_inc(s_prm, 1)
                m += 1
                dve.wait_ge(s_prm, m)

            step_bits = float(2 ** 23)
            by_tensor = "p (e u) -> p e u"
            plink(dve.tensor_scalar(w_inv[:], half_exp[:], step_bits, float((65 - TOP_EXP) * 2 ** 23), ALU.mult, ALU.add))
            plink(dve.tensor_scalar(hq[:], b1fro[:], 2.0, None, ALU.mult))
            plink(dve.scalar_tensor_tensor(out=hq[:], in0=fro[:].rearrange(by_tensor, u=2)[:, :, 0], scalar=2.0 * D, in1=hq[:],
                                           op0=ALU.mult, op1=ALU.add))
            plink(dve.tensor_scalar(h_half[:], hq[:].bitcast(I32), 24, None, ALU.logical_shift_right))
            plink(dve.tensor_scalar(h_scale[:], h_half[:], -step_bits, float((189 + TOP_EXP) * 2 ** 23), ALU.mult, ALU.add))
            plink(dve.tensor_scalar(h_inv[:], h_half[:], step_bits, float((65 - TOP_EXP) * 2 ** 23), ALU.mult, ALU.add))
            inv = w_inv[:].bitcast(F32).rearrange(by_tensor, u=2)
            plink(dve.tensor_tensor(scaleA[:], h_scale[:].bitcast(F32), inv[:, :, 0], ALU.mult))
            plink(dve.tensor_tensor(scaleY[:], h_inv[:].bitcast(F32), inv[:, :, 1], ALU.mult))
            hs = h_scale[:].bitcast(F32)
            dve.tensor_tensor(biasA[:], b1T, hs.unsqueeze(2).to_broadcast([P, E, KI]), ALU.mult).then_inc(s_param, 1)

            dve.wait_ge(s_ids, 16)
            R = SLOT_TILES
            link(dve.tensor_scalar(tok_i[0:R, 0], ids[0:R, :], 1, None, ALU.logical_shift_right))
            link(dve.tensor_scalar(tok_i[0:R, 1], ids[0:R, :], 1, None, ALU.bitwise_and))
            link(dve.tensor_copy(tok_f[0:R, 0], tok_i[0:R, 0]))
            link(dve.tensor_copy(tok_f[0:R, 2], tok_i[0:R, 1]))
            link(dve.tensor_scalar(beyond[0:R, :], iota_f[0:R, :], tcol[0:R, 1:2], 2.0 * N, ALU.is_ge, ALU.mult))
            dve.tensor_tensor(tok_f[0:R, 1], tok_f[0:R, 0], beyond[0:R, :], ALU.add).then_inc(s_tokf, 1)
            dve.wait_ge(s_tabT, 1)
            link(dve.tensor_copy(tile_src[:], bank[4][:, 0:R]))
            link(dve.tensor_copy(tile_dst[:], bank[4][:, 64:64 + R]))
            link(dve.tensor_copy(tile_choice[:], bank[4][:, 128:128 + R]))
            dve.tensor_copy(tile_expert[:], bank[4][0:1, 192:192 + R]).then_inc(s_table, 1)
            dve.wait_ge(s_table, 1)
            dve.wait_ge(s_b2, 16)

            def rows_turned(t, u):
                wait(dve, s_xgT, t + 1)
                wait(dve, s_mm1[1], t - 1)
                dve.tensor_copy(xgT[:, u], bank[0][:, 0:2 * P].bitcast(F16).rearrange("p (j s) -> p j s", s=P)).then_inc(s_xgc, 1)
                meta = xg[:, u, D:ROW]
                dve.scalar_tensor_tensor(out=gate[:, bass.ds(t, 1)], in0=meta[:, 1:2], scalar=tile_choice[:, bass.ds(t, 1)],
                                         in1=meta[:, 0:1], op0=ALU.mult, op1=ALU.add).then_inc(s_wsel, 1)

            def rows_out(t, u):
                e = dve.value_load(tile_expert[0:1, bass.ds(t, 1)], min_val=0, max_val=E - 1)
                wait(dve, s_mm2, t + 1)
                wait(dve, s_yg, t)
                dve.scalar_tensor_tensor(out=y32, in0=bank[5 + u][:, 0:D], scalar=scaleY[:, bass.ds(e, 1)],
                                         in1=b2_all[:, bass.ds(e, 1)].rearrange("p a d -> p (a d)"),
                                         op0=ALU.mult, op1=ALU.add).then_inc(s_y32, 1)
                wait(dve, s_y32, t + 1)
                wait(dve, s_wsel, t + 1)
                if not isinstance(t, int) or t >= 2:
                    wait(dve, s_add, (t - 1) * 16)
                dve.tensor_scalar(yg[:, u], y32, gate[:, bass.ds(t, 1)], None, ALU.mult).then_inc(s_yg, 1)

            rows_turned(0, 0)

            def step(t, u, k):
                for half in range(2):
                    part = slice(4 * half, 4 * half + 4)
                    wait(dve, s_act[half], t + 1)
                    wait(dve, s_mm2, t - 1)
                    dve.tensor_copy(hid_h[:, u, part], act32[:, part]).then_inc(s_hidh[half], 1)
                    wait(dve, s_hidh[half], t + 1)
                    dve.tensor_tensor(hid_l[:, u, part], act32[:, part], hid_h[:, u, part], ALU.subtract).then_inc(s_hidl[half], 1)
                if not isinstance(t, int) or t < SLOT_TILES - 1:
                    rows_turned(t + 1, 1 - u)
                if not isinstance(t, int) or t >= 1:
                    rows_out(t - 1, 1 - u)

            slot_steps(dve, step)
            rows_out(SLOT_TILES - 1, 0)

        @block.tensor
        def _(pe):
            pe.wait_ge(s_const, 14)
            pe.wait_ge(s_small, 96)
            pe.transpose(bank[7][:, 0:NB], b_rows, ident_f[0:NB, 0:NB]).then_inc(s_b1T, 1)
            pe.wait_ge(s_wself, 32)
            for src, dst in ((raw_self, bank[2]), (raw_nb, bank[3])):
                for kb in range(KD):
                    for ka in range(KD):
                        at = kb * D + ka * P
                        ins = pe.transpose(dst[:, at:at + P], src[:, ka, kb * P:(kb + 1) * P], ident_f[:])
                ins.then_inc(s_setT, 1)
            pe.wait_ge(s_wcomb, 16)
            for i, (src, dst) in enumerate(((selfT, bank[4]), (nbT, bank[5]))):
                pe.wait_ge(s_setTc, i + 1)
                for ka in range(KD):
                    for kb in range(KD):
                        ins = pe.matmul(dst[:, ka * D:(ka + 1) * D], src[:, kb, ka * P:(ka + 1) * P], raw_comb[:, i * KD + kb],
                                        start=(kb == 0), stop=(kb == KD - 1))
                ins.then_inc(s_setP, 1)
            pe.wait_ge(s_bcols, 2 * KD)
            for i in range(2 * KD):
                ins = pe.matmul(bank[6][:, 0:D], bias_cols[:, i], raw_comb[:, i], start=(i == 0), stop=(i == 2 * KD - 1))
            ins.then_inc(s_setP, 1)
            pe.wait_ge(s_setPc, 2)
            pe.wait_ge(s_bias, 1)
            pe.wait_ge(s_b1q, 1)

            def aggregate(s, u, half):
                for j in range(HJ * half, HJ * (half + 1)):
                    if isinstance(s, int) and s == 0 and j % 4 == 0:
                        pe.wait_ge(s_xl, j // 4 + 1)
                    pe.matmul(agg_ps[u][:, 0:D + 1], maskT[:, u, j], XH[:, j, 0:D + 1], start=(j == 0), stop=False)
                    ins = pe.matmul(agg_ps[u][:, 0:D], maskT[:, u, j], XL[:, j], start=False, stop=(j == NT - 1))
                return ins

            def step(s, u, k):
                if is_step(s, 0, NT - 1):
                    wait(pe, s_adj[u], 16 * (k + 1))
                    for half in range(2):
                        wait(pe, s_mask[half], s)
                        for j in range(HJ):
                            at = (half * HJ + j) * P
                            ins = pe.transpose(mask_ps[half][:, j], adj_rows[:, u, at:at + P], ident_b[:])
                        ins.then_inc(s_tr[half], 1)
                if is_step(s, 1, NT):
                    wait(pe, s_aggn, s)
                    wait(pe, s_x32, s)
                    wait(pe, s_ctc, s - 1)
                    for i, src in enumerate((aggn, x32)):
                        for kd in range(KD):
                            ins = pe.transpose(trx_ps[:, i * KD + kd], src[:, kd * P:(kd + 1) * P], ident_f[:])
                    ins.then_inc(s_ct, 1)
                if is_step(s, 2, LAST):
                    wait(pe, s_h, s - 1)
                    wait(pe, s_htc, s - 2)
                    for kd in range(KD):
                        ins = pe.transpose(hT_ps[:, kd], h32[:, kd * P:(kd + 1) * P], ident_f[:])
                    ins.then_inc(s_ht, 1)
                if is_step(s, 0, NT - 1):
                    wait(pe, s_mask[0], s + 1)
                    wait(pe, s_aggn, s - 1)
                    aggregate(s, u, 0)
                if is_step(s, 2, LAST):
                    wait(pe, s_htc, s - 1)
                    wait(pe, s_dest, s - 2)
                    for kd in range(KD):
                        ins = pe.matmul(lg_ps, hT[:, kd], gw[:, kd], start=(kd == 0), stop=(kd == KD - 1))
                    ins.then_inc(s_lg, 1)
                if is_step(s, 1, NT):
                    wait(pe, s_ctc, s)
                    wait(pe, s_prec, s - 1)
                    for i in range(2 * KD):
                        prod = wn_prod if i < KD else ws_prod
                        ins = pe.matmul(pre_ps, cT[:, i], prod[:, i % KD], start=(i == 0), stop=(i == 2 * KD - 1))
                    ins.then_inc(s_pre, 1)
                if is_step(s, 2, LAST):
                    wait(pe, s_chosen, s - 1)
                    pe.matmul(rank_ps, before[:], chosen[:], start=True, stop=False)
                    pe.matmul(rank_ps, ones_b[:], chosen_sum[:], start=False, stop=True).then_inc(s_rank, 1)
                if is_step(s, 0, NT - 1):
                    wait(pe, s_mask[1], s + 1)
                    aggregate(s, u, 1).then_inc(s_agg, 1)

            graph_steps(pe, step)

            pe.wait_ge(s_dest, NT)
            pe.matmul(cnt_ps, ones_b[:], chosen_sum[:], start=True, stop=True).then_inc(s_cnt, 1)
            pe.wait_ge(s_tokf, 1)
            R = SLOT_TILES
            for i in range(3):
                pe.transpose(bank[4][:, 64 * i:64 * i + R], tok_f[0:R, i], ident_f[0:R, 0:R])
            pe.transpose(bank[4][0:1, 192:192 + R], tcol[0:R, 2:3], ident_f[0:R, 0:R]).then_inc(s_tabT, 1)

            def turn_rows(t, u, k):
                wait(pe, s_xg[u], 16 * (k + 1))
                wait(pe, s_xgc, t)
                for j in range(4):
                    ins = pe.transpose(bank[0][:, 64 * j:64 * (j + 1)].bitcast(F16), xg[:, u, j * 64:(j + 1) * 64].bitcast(F16), ident_h[:])
                ins.then_inc(s_xgT, 1)

            def up(t, u):
                e = pe.value_load(tile_expert[0:1, bass.ds(t, 1)], min_val=0, max_val=E - 1)
                wait(pe, s_xgc, t + 1)
                for half in range(2):
                    wait(pe, s_act[half], t - 1)
                    for c in range(4 * half, 4 * half + 4):
                        dst = bank[1 + 2 * u + half][:, (c % 4) * P:(c % 4 + 1) * P]
                        for kd in range(KD):
                            cols = slice(c * P, (c + 1) * P)
                            hi = W1H[:, bass.ds(e, 1), kd, cols].rearrange("p a i -> p (a i)")
                            lo = W1L[:, bass.ds(e, 1), kd, cols].rearrange("p a i -> p (a i)")
                            pe.matmul(dst, hi, xgT[:, u, kd], start=(kd == 0), stop=False)
                            pe.matmul(dst, hi, xgT[:, u, KD + kd], start=False, stop=False)
                            ins = pe.matmul(dst, lo, xgT[:, u, kd], start=False, stop=(kd == KD - 1))
                    ins.then_inc(s_mm1[half], 1)

            def down(t, u):
                e = pe.value_load(tile_expert[0:1, bass.ds(t, 1)], min_val=0, max_val=E - 1)
                wait(pe, s_y32, t - 1)
                dst = bank[5 + u][:, 0:D]
                for c in range(KI):
                    if c % 4 == 0:
                        wait(pe, s_hidl[c // 4], t + 1)
                    hi = W2H[:, bass.ds(e, 1), c].rearrange("p a d -> p (a d)")
                    lo = W2L[:, bass.ds(e, 1), c].rearrange("p a d -> p (a d)")
                    pe.matmul(dst, hid_h[:, u, c], hi, start=(c == 0), stop=False)
                    pe.matmul(dst, hid_h[:, u, c], lo, start=False, stop=False)
                    ins = pe.matmul(dst, hid_l[:, u, c], hi, start=False, stop=(c == KI - 1))
                ins.then_inc(s_mm2, 1)

            pe.wait_ge(s_wlo, NT)
            pe.wait_ge(s_table, 1)
            turn_rows(0, 0, 0)

            def step(t, u, k):
                up(t, u)
                if not isinstance(t, int) or t < SLOT_TILES - 1:
                    turn_rows(t + 1, 1 - u, k + u)
                if not isinstance(t, int) or t >= 1:
                    down(t - 1, 1 - u)

            slot_steps(pe, step)
            down(SLOT_TILES - 1, 0)


_INS = ['x', 'adj', 'L0_gnn_W_self', 'L0_gnn_b_self', 'L0_gnn_W_nb', 'L0_gnn_b_nb', 'L0_gnn_W_comb', 'L0_gnn_b_comb',
        'L0_ffn_gate_w', 'L0_ffn_gate_b', 'L0_ffn_w1', 'L0_ffn_b1', 'L0_ffn_w2', 'L0_ffn_b2']
_OUTS = [((2048, 256), 'float32')]


def kernel(**inputs):
    import numpy as _np
    import concourse.bacc as _bacc
    from concourse import mybir as _mybir
    from concourse.bass_utils import run_bass_kernel_spmd as _run

    nc = _bacc.Bacc("TRN2", target_bir_lowering=False, num_devices=1)
    arrays, args = {}, []
    for name in _INS:
        a = _np.ascontiguousarray(inputs[name])
        arrays[f"in_{name}_dram"] = a
        args.append(nc.dram_tensor(f"in_{name}_dram", a.shape, _mybir.dt.from_np(a.dtype), kind="ExternalInput").ap())
    for i, (shape, dtype) in enumerate(_OUTS):
        dt = _mybir.dt.from_np(_np.dtype(dtype))
        args.append(nc.dram_tensor(f"out_{i}_dram", shape, dt, kind="ExternalOutput").ap())
    gnn_moe_kernel(nc, *args)
    r = _run(nc, [arrays], core_ids=[0])
    got = tuple(r.results[0][f"out_{i}_dram"] for i in range(len(_OUTS)))
    return got[0]
```

```python
from contextlib import ExitStack

import concourse.bass as bass
from concourse import mybir

F32 = mybir.dt.float32
F16 = mybir.dt.float16
BF16 = mybir.dt.bfloat16
I32 = mybir.dt.int32
U32 = mybir.dt.uint32
ALU = mybir.AluOpType
ACT = mybir.ActivationFunctionType
AX = mybir.AxisListType.X
RADD = bass.bass_isa.ReduceOp.add
AT = bass.IndirectOffsetOnAxis

P = 128
EPS = 1e-5
TOP_EXP = 15


def wait(eng, sem, value):
    if isinstance(value, int) and value <= 0:
        return
    eng.wait_ge(sem, value)


def gnn_moe_kernel(nc, x, adj, w_self, b_self, w_nb, b_nb, w_comb, b_comb,
                   gate_w, gate_b, w1, b1, w2, b2, out):
    N, D = x.shape
    E, _, I = w1.shape
    KD = D // P
    KI = I // P
    NT = N // P
    HJ = NT // 2
    SLOT_TILES = (2 * N + E * (P - 1)) // P
    BLOCKS = N // P
    ROW = D + 2
    assert NT == 2 * E and BLOCKS * E == P and KD == 2

    hrows = nc.dram_tensor("hrows", [N, ROW], F32, kind="Internal").ap()
    idtab = nc.dram_tensor("idtab", [P, P], I32, kind="Internal").ap()
    idtab_flat = idtab.rearrange("b (s a) -> (b s) a", a=1)

    with ExitStack() as ctx:
        def sb(name, shape, dt):
            return ctx.enter_context(nc.sbuf_tensor(name, shape, dt))

        def psum(name, shape, dt):
            return ctx.enter_context(nc.psum_tensor(name, shape, dt))

        def sem(name):
            return ctx.enter_context(nc.semaphore(name))

        W1H = sb("W1H", [P, E, KD, I], F16)
        W1L = sb("W1L", [P, E, KD, I], F16)
        W2S = sb("W2S", [P, E, KI, 2 * D], F16)
        XH = sb("XH", [P, NT, D + 2], F16)
        XL = sb("XL", [P, NT, D], F16)
        adj_rows = sb("adj_rows", [P, 2, N], BF16)
        w_stage = sb("w_stage", [P, 2, KD * I], F32)
        maskT = sb("maskT", [P, 2, NT, P], F16)

        scr1 = W1L[:, E // 2:E].rearrange("p e k i -> p (e k i)").bitcast(F32)
        scr2 = W2S[:, 3 * E // 4:E].rearrange("p e k i -> p (e k i)").bitcast(F32)
        x0 = scr2.rearrange("p (t d) -> p t d", d=D)
        raw_self = scr1[:, 0:512].rearrange("p (k d) -> p k d", k=KD)
        raw_nb = scr1[:, 512:1024].rearrange("p (k d) -> p k d", k=KD)
        raw_comb = scr1[:, 1024:2048].rearrange("p (k d) -> p k d", k=2 * KD)
        selfT = scr1[:, 2048:2560].rearrange("p (k d) -> p k d", k=KD)
        nbT = scr1[:, 2560:3072].rearrange("p (k d) -> p k d", k=KD)
        bias_cols = scr1[:, 3072:3584].rearrange("p (k m) -> p k m", k=2 * KD)
        NB = E * KI + 2 * KD
        b_rows = scr1[0:NB, 3584:3712]
        b1sq = scr1[:, 3776:3840]

        ws_prod = sb("ws_prod", [P, KD, D], F32)
        wn_prod = sb("wn_prod", [P, KD, D], F32)
        bias = sb("bias", [P, D], F32)
        gw = sb("gw", [P, KD, E], F32)
        gb = sb("gb", [P, E], F32)
        bT = sb("bT", [P, NB], F32)
        b1T = bT[:, 0:E * KI].rearrange("p (e c) -> p e c", e=E)
        ident_f = sb("ident_f", [P, P], F32)
        ident_b = sb("ident_b", [P, P], BF16)
        ident_h = sb("ident_h", [P, P], F16)
        before = sb("before", [P, P], BF16)
        ones_b = sb("ones_b", [P, P], BF16)
        iota_e = sb("iota_e", [P, E], F32)
        expert_base = sb("expert_base", [P, E], F32)
        iota_p = sb("iota_p", [P, 1], F32)
        iota_f = sb("iota_f", [P, P], F32)
        slot_ids = sb("slot_ids", [P, NT * 2], I32)
        zero_ids = sb("zero_ids", [P, P], I32)
        minus_half = sb("minus_half", [P, NT], F32)

        ln_stat = sb("ln_stat", [P, NT, 6], F32)
        ln_mv = sb("ln_mv", [P, NT, 2], F32)
        ln_ve = sb("ln_ve", [P, NT], F32)
        ln_rs = sb("ln_rs", [P, NT], F32)
        mean_nb = sb("mean_nb", [P, D], F32)
        cT = sb("cT", [P, 4, P], F32)
        pre = sb("pre", [P, D], F32)
        x1 = sb("x1", [P, 2, D], F32)
        h32 = sb("h32", [P, D], F32)
        hT = sb("hT", [P, KD, P], F32)
        hrow = sb("hrow", [P, 2, ROW], F32)
        deg = sb("deg", [P, 2], F32)
        rdeg = sb("rdeg", [P, 2], F32)
        st2 = sb("st2", [P, 6], F32)
        mv2 = sb("mv2", [P, 2, 2], F32)
        ve2 = sb("ve2", [P, 2], F32)
        rs2 = sb("rs2", [P, 2], F32)
        lg = sb("lg", [P, E], F32)
        lmax = sb("lmax", [P, 1], F32)
        lshift = sb("lshift", [P, E], F32)
        pexp = sb("pexp", [P, E], F32)
        psum_e = sb("psum_e", [P, 1], F32)
        prec = sb("prec", [P, 1], F32)
        prob = sb("prob", [P, E], F32)
        top = sb("top", [P, 8], F32)
        top_i = sb("top_i", [P, 8], U32)
        top_f = sb("top_f", [P, 2], F32)
        vdiff = sb("vdiff", [P, 1], F32)
        ediff = sb("ediff", [P, 1], F32)
        eplus = sb("eplus", [P, 1], F32)
        gate0 = sb("gate0", [P, 1], F32)
        pick = sb("pick", [P, 2, 2, E], F32)
        chosen = sb("chosen", [P, 2, E], BF16)
        chosen_sum = sb("chosen_sum", [P, E], BF16)
        place = sb("place", [P, E], F32)
        pjunk = sb("pjunk", [P, 2, E], F32)
        dest = sb("dest", [P, 2], F32)
        dest_i = sb("dest_i", [P, 2, 2], I32)
        ssq = sb("ssq", [P, 2], F32)
        fro_now = sb("fro_now", [P, 2], F32)
        fro = sb("fro", [P, 2 * E], F32)
        half_exp = sb("half_exp", [P, 2 * E], I32)
        w_scale = sb("w_scale", [P, 2 * E], I32)
        w_inv = sb("w_inv", [P, 2 * E], I32)
        b1q = sb("b1q", [P, E], F32)
        b1fro = sb("b1fro", [P, E], F32)
        hq = sb("hq", [P, E], F32)
        h_half = sb("h_half", [P, E], I32)
        h_scale = sb("h_scale", [P, E], I32)
        h_inv = sb("h_inv", [P, E], I32)
        scaleA = sb("scaleA", [P, E], F32)
        biasA = sb("biasA", [P, E, KI], F32)
        scaleY = sb("scaleY", [P, E], F32)

        cnt = sb("cnt", [P, E], F32)
        cnt_i = sb("cnt_i", [P, E], I32)
        tiles_i = sb("tiles_i", [P, E], I32)
        ntile = sb("ntile", [P, E], F32)
        pfx = sb("pfx", [P, 3, E], F32)
        start_t = sb("start_t", [P, E], F32)
        past = sb("past", [P, E], F32)
        owns = sb("owns", [P, E], F32)
        local = sb("local", [P, E], F32)
        blk = sb("blk", [P, E], F32)
        left = sb("left", [P, E], F32)
        tjunk = sb("tjunk", [P, 3, E], F32)
        tcol = sb("tcol", [P, 3], F32)
        blk_i = sb("blk_i", [P, 1], I32)
        expert_blk = sb("expert_blk", [P, E], F32)
        ids = sb("ids", [P, P], I32)
        tok_i = sb("tok_i", [P, 2, P], I32)
        tok_f = sb("tok_f", [P, 3, P], F32)
        beyond = sb("beyond", [P, P], F32)
        tile_src = sb("tile_src", [P, SLOT_TILES], I32)
        tile_dst = sb("tile_dst", [P, SLOT_TILES], I32)
        ids_now = sb("ids_now", [P, 2, 2], I32)
        src_now = sb("src_now", [P, 2], I32)
        dst_now = sb("dst_now", [P, 2], I32)
        tile_choice = sb("tile_choice", [P, SLOT_TILES], F32)
        tile_expert = sb("tile_expert", [1, SLOT_TILES], I32)

        ws_flat = w_stage[:].rearrange("p u n -> p (u n)")
        act32 = ws_flat[:, 0:KI * P].rearrange("p (c s) -> p c s", c=KI)
        hid_h = ws_flat[:, 1024:2048].bitcast(F16).rearrange("p (b c s) -> p b c s", b=2, c=KI)
        hid_l = ws_flat[:, 2048:3072].bitcast(F16).rearrange("p (b c s) -> p b c s", b=2, c=KI)
        b2_all = adj_rows[:].rearrange("p u n -> p (u n)").bitcast(F32).rearrange("p (e d) -> p e d", e=E)
        XL_flat = XL[:].rearrange("p t d -> p (t d)")
        mt_flat = maskT[:].rearrange("p u j s -> p (u j s)")
        xg = mt_flat[:, 0:4 * ROW].bitcast(F32).rearrange("p (b d) -> p b d", b=2)
        xgT = mt_flat[:, 2080:3104].rearrange("p (b j s) -> p b j s", b=2, j=4)
        yg = XL_flat[:, 0:1024].bitcast(F32).rearrange("p (b d) -> p b d", b=2)
        y32 = XL_flat[:, 1024:1536].bitcast(F32)
        gate = sb("gate", [P, SLOT_TILES], F32)

        bank = [psum(f"bank{i}", [P, 512], F32) for i in range(8)]
        mask_ps = [bank[i][:].bitcast(BF16).rearrange("p (j s) -> p j s", s=P) for i in range(2)]
        agg_ps = [bank[2], bank[3]]
        deg_ps = bank[4][:, 0:1]
        pre_ps = bank[5]
        hT_ps = bank[6][:, 0:D].rearrange("p (k s) -> p k s", s=P)
        lg_ps = bank[7][:, 0:E]
        rank_ps = bank[4][:, 16:16 + E]
        cnt_ps = bank[7][:, 32:32 + E]

        s_xin = [sem(f"s_xin{g}") for g in range(4)]
        s_wself = sem("s_wself")
        s_wcomb = sem("s_wcomb")
        s_small = sem("s_small")
        s_const = sem("s_const")
        s_set = sem("s_set")
        s_rstd = sem("s_rstd")
        s_xn = sem("s_xn")
        s_xh = sem("s_xh")
        s_xl = sem("s_xl")
        s_setT = sem("s_setT")
        s_setTc = sem("s_setTc")
        s_setP = sem("s_setP")
        s_setPc = sem("s_setPc")
        s_bcols = sem("s_bcols")
        s_bias = sem("s_bias")
        s_b1T = sem("s_b1T")
        s_b1q = sem("s_b1q")
        s_b1f = sem("s_b1f")
        s_gps = sem("s_gps")
        s_idz = sem("s_idz")

        s_adj = [sem(f"s_adj{u}") for u in range(2)]
        s_w = [sem(f"s_w{u}") for u in range(2)]
        s_x = [sem(f"s_xrow{u}") for u in range(2)]
        s_x1st = [sem(f"s_x1st{u}") for u in range(2)]
        s_hst = [sem(f"s_hst{u}") for u in range(2)]
        s_idst = [sem(f"s_idst{u}") for u in range(2)]
        s_tr = [sem("s_trA"), sem("s_trB")]
        s_mask = [sem("s_maskA"), sem("s_maskB")]
        s_agg = sem("s_agg")
        s_deg = sem("s_deg")
        s_rdeg = sem("s_rdeg")
        s_nb = sem("s_nb")
        s_ctc = sem("s_ctc")
        s_pre = sem("s_pre")
        s_prec = sem("s_prec")
        s_x1 = sem("s_x1")
        s_ln = sem("s_ln")
        s_ve = sem("s_ve")
        s_rs = sem("s_rs")
        s_h = sem("s_h")
        s_ht = sem("s_ht")
        s_htc = sem("s_htc")
        s_lg = sem("s_lg")
        s_lgc = sem("s_lgc")
        s_slot = sem("s_slot")
        s_gate = sem("s_gate")
        s_shift = sem("s_shift")
        s_pexp = sem("s_pexp")
        s_vdiff = sem("s_vdiff")
        s_ediff = sem("s_ediff")
        s_meta = sem("s_meta")
        s_chosen = sem("s_chosen")
        s_rank = sem("s_rank")
        s_dest = sem("s_dest")
        s_hlo = sem("s_hlo")
        s_hhi = sem("s_hhi")
        s_sq = sem("s_sq")
        s_fro = sem("s_fro")
        s_scl = sem("s_scl")
        s_frc = sem("s_frc")
        s_scale = sem("s_scale")
        s_whi = sem("s_whi")
        s_wlo = sem("s_wlo")

        s_cnt = sem("s_cnt")
        s_tab = sem("s_tab")
        s_blk = sem("s_blk")
        s_ids = sem("s_ids")
        s_tokf = sem("s_tokf")
        s_tabT = sem("s_tabT")
        s_table = sem("s_table")
        s_prm = sem("s_prm")
        s_param = sem("s_param")
        s_b2 = sem("s_b2")

        s_xg = [sem(f"s_xg{u}") for u in range(2)]
        s_src = sem("s_src")
        s_idn = sem("s_idn")
        s_dst = sem("s_dst")
        s_xgT = sem("s_xgT")
        s_xgc = sem("s_xgc")
        s_wsel = sem("s_wsel")
        s_gt = sem("s_gt")
        s_mm1 = [sem("s_mm1A"), sem("s_mm1B")]
        s_act = [sem("s_actA"), sem("s_actB")]
        s_hidh = [sem("s_hidhA"), sem("s_hidhB")]
        s_hidl = [sem("s_hidlA"), sem("s_hidlB")]
        s_mm2 = sem("s_mm2")
        s_ylo = sem("s_ylo")
        s_y32 = sem("s_y32")
        s_yg = sem("s_yg")
        s_add = sem("s_add")

        x_t = x.rearrange("(t p) d -> t p d", p=P)
        out_t = out.rearrange("(t p) d -> t p d", p=P)
        adj_t = adj.rearrange("(t p) j -> t p j", p=P)
        hrows_t = hrows.rearrange("(t p) d -> t p d", p=P)
        w1_t = w1.rearrange("e (k p) i -> e p k i", p=P)
        w2_t = w2.rearrange("e (c p) d -> e p c d", p=P)

        def stage_w(u):
            return w_stage[:, u].rearrange("p (k i) -> p k i", k=KD if u == 0 else KI)

        def wsplit(u, e):
            if u == 0:
                hi, lo = W1H[:, e], W1L[:, e]
            else:
                hi, lo = W2S[:, e, :, 0:D], W2S[:, e, :, D:2 * D]
            return hi.rearrange("p a k i -> p (a k) i"), lo.rearrange("p a k i -> p (a k) i")

        ROUTE_LAST = NT + 1
        RANK_LAST = NT + 2
        LAST = NT + 3

        def graph_steps(eng, step):
            for s in range(6):
                step(s, s % 2, s // 2)
            with eng.Fori(0, NT // 2 - 5) as q:
                for u in range(2):
                    step(q * 2 + (6 + u), u, q + 3)
            for s in range(NT - 4, LAST + 1):
                step(s, s % 2, s // 2)

        def is_step(s, lo, hi):
            return not isinstance(s, int) or lo <= s <= hi

        def slot_steps(eng, step, new_round=None, rounds=(SLOT_TILES - 3) // 4, end=SLOT_TILES):
            step(0, 0, 0)
            step(1, 1, 0)
            with eng.Fori(0, rounds) as q:
                if new_round:
                    new_round()
                for j in range(4):
                    step(q * 4 + (2 + j), j % 2, q * 2 + (1 + j // 2))
            if new_round:
                new_round()
            for t in range(2 + 4 * rounds, end):
                step(t, t % 2, t // 2)

        assert SLOT_TILES % 4 == 3

        block = ctx.enter_context(nc.Block())

        @block.sync
        def _(sp):
            for g in range(4):
                sp.dma_start(x0[:, 4 * g:4 * g + 4], x_t[4 * g:4 * g + 4].rearrange("t p d -> p t d")).then_inc(s_xin[g], 16)
            sp.dma_start(raw_self, w_self.rearrange("(k p) d -> p k d", p=P)).then_inc(s_wself, 16)
            sp.dma_start(raw_nb, w_nb.rearrange("(k p) d -> p k d", p=P)).then_inc(s_wself, 16)
            sp.dma_start(raw_comb, w_comb.rearrange("(k p) d -> p k d", p=P)).then_inc(s_wcomb, 16)
            sp.dma_start(b_rows[E * KI:E * KI + KD, :], b_self.rearrange("(k p) -> k p", p=P)).then_inc(s_small, 16)
            sp.dma_start(b_rows[E * KI + KD:NB, :], b_nb.rearrange("(k p) -> k p", p=P)).then_inc(s_small, 16)
            sp.dma_start(bias[:], b_comb.partition_broadcast(P)).then_inc(s_small, 16)
            sp.dma_start(gw[:], gate_w.rearrange("(k p) e -> p k e", p=P)).then_inc(s_small, 16)
            sp.dma_start(gb[:], gate_b.partition_broadcast(P)).then_inc(s_small, 16)
            sp.dma_start(b_rows[0:E * KI, :], b1.rearrange("e (c p) -> (e c) p", p=P)).then_inc(s_small, 16)

            def load_w(i, u, k):
                src = w1_t if u == 0 else w2_t
                e = k
                sp.dma_start(stage_w(u), src[bass.ds(e, 1)].rearrange("a p k i -> p (a k) i")).then_inc(s_w[u], 16)

            load_w(0, 0, 0)
            load_w(1, 1, 0)

            def step(s, u, k):
                if is_step(s, 0, NT - 1):
                    wait(sp, s_h, s - 1)
                    wait(sp, s_x1st[u], 16 * k)
                    sp.dma_start(x1[:, u], x_t[bass.ds(s, 1)].rearrange("t p d -> p (t d)")).then_inc(s_x[u], 16)
                if is_step(s, 1, NT - 2):
                    wait(sp, s_wlo, s)
                    load_w(s + 1, 1 - u, k + u)
                if is_step(s, 1, NT):
                    wait(sp, s_x1, s)
                    sp.dma_start(out_t[bass.ds(s - 1, 1)].rearrange("t p d -> p (t d)"), x1[:, 1 - u]).then_inc(s_x1st[1 - u], 16)
                if is_step(s, 2, ROUTE_LAST):
                    wait(sp, s_hlo, s - 1)
                    wait(sp, s_meta, s - 1)
                    sp.dma_start(hrows_t[bass.ds(s - 2, 1)].rearrange("t p d -> p (t d)"), hrow[:, u]).then_inc(s_hst[u], 16)

            graph_steps(sp, step)
            sp.wait_ge(s_tr[1], NT)
            sp.dma_start(b2_all, b2.rearrange("e d -> (e d)").partition_broadcast(P).rearrange("p (e d) -> p e d", e=E)).then_inc(s_b2, 16)

        @block.gpsimd
        def _(pool):
            for t in (ident_f, ident_b, ident_h):
                pool.memset(t[:], 0.0).then_inc(s_gps, 1)
            pool.memset(before[:], 1.0).then_inc(s_gps, 1)
            pool.memset(zero_ids[:], 0).then_inc(s_gps, 1)
            pool.wait_ge(s_gps, 5)
            pool.dma_start(idtab, zero_ids[:]).then_inc(s_idz, 16)

            def load_adj(s, u):
                pool.dma_start(adj_rows[:, u], adj_t[bass.ds(s, 1)].rearrange("t p j -> p (t j)")).then_inc(s_adj[u], 16)

            load_adj(0, 0)
            load_adj(1, 1)
            for t in (ident_f, ident_b, ident_h):
                pool.affine_select(out=t[:], in_=t[:], compare_op=ALU.not_equal, fill=1.0, base=0,
                                   pattern=[[-1, P]], channel_multiplier=1).then_inc(s_const, 1)
            pool.affine_select(out=before[:], in_=before[:], compare_op=ALU.is_gt, fill=0.0, base=0,
                               pattern=[[1, P]], channel_multiplier=-1).then_inc(s_const, 1)
            pool.memset(ones_b[:], 1.0).then_inc(s_const, 1)
            pool.memset(XH[:, :, D:D + 2], 1.0).then_inc(s_const, 1)
            pool.memset(chosen_sum[:], 0.0).then_inc(s_const, 1)
            pool.memset(minus_half[:], -0.5).then_inc(s_const, 1)
            pool.iota(iota_e[:], pattern=[[1, E]], base=0, channel_multiplier=0, allow_small_or_imprecise_dtypes=True).then_inc(s_const, 1)
            pool.iota(expert_base[:], pattern=[[N, E]], base=0, channel_multiplier=0, allow_small_or_imprecise_dtypes=True).then_inc(s_const, 1)
            pool.iota(expert_blk[:], pattern=[[BLOCKS, E]], base=0, channel_multiplier=0, allow_small_or_imprecise_dtypes=True).then_inc(s_const, 1)
            pool.iota(iota_p[:], pattern=[[0, 1]], base=0, channel_multiplier=1, allow_small_or_imprecise_dtypes=True).then_inc(s_const, 1)
            pool.iota(iota_f[:], pattern=[[1, P]], base=0, channel_multiplier=0, allow_small_or_imprecise_dtypes=True).then_inc(s_const, 1)
            pool.iota(slot_ids[:].rearrange("p (t c) -> p t c", c=2), pattern=[[2 * P, NT], [1, 2]], base=0, channel_multiplier=2).then_inc(s_const, 1)
            pool.wait_ge(s_const, 14)
            pool.wait_ge(s_set, NT + NT + 1)
            pool.tensor_tensor(ln_rs[:], ln_ve[:], minus_half[:], ALU.pow).then_inc(s_rstd, 1)
            pool.wait_ge(s_b1q, 2)
            pool.partition_all_reduce(b1fro[:], b1q[:], P, RADD).then_inc(s_b1f, 1)
            pool.wait_ge(s_xl, 4)
            pool.wait_ge(s_xh, 4)
            pool.wait_ge(s_idz, 16)

            pool.wait_ge(s_tr[1], 1)
            load_adj(2, 0)

            def step(s, u, k):
                if is_step(s, 4, LAST):
                    wait(pool, s_dest, s - 3)
                    pool.nop(nofuse=True)
                    pool.tensor_copy(ids_now[:, u], slot_ids[:, bass.ds((s - 4) * 2, 2)]).then_inc(s_idn, 1)
                    wait(pool, s_idn, s - 3)
                    pool.nop(nofuse=True)
                    for c in range(2):
                        pool.indirect_dma_start(out=idtab_flat, out_offset=AT(ap=dest_i[:, u, c:c + 1], axis=0),
                                                in_=ids_now[:, u, c:c + 1], in_offset=None).then_inc(s_idst[u], 16)
                if is_step(s, 2, ROUTE_LAST):
                    wait(pool, s_hst[u], 16 * (k - 1))
                    pool.nop(nofuse=True)
                    wait(pool, s_h, s - 1)
                    pool.nop(nofuse=True)
                    halves = hrow[:, u, 0:D].bitcast(F16)
                    pool.tensor_copy(halves[:, 0:D], h32[:]).then_inc(s_hhi, 1)
                    wait(pool, s_hhi, s - 1)
                    pool.nop(nofuse=True)
                    pool.tensor_tensor(halves[:, D:2 * D], h32[:], halves[:, 0:D], ALU.subtract).then_inc(s_hlo, 1)
                if is_step(s, 0, NT - 4):
                    wait(pool, s_tr[1], s + 2)
                    pool.nop(nofuse=True)
                    load_adj(s + 3, 1 - u)
                if is_step(s, 0, NT - 1):
                    wait(pool, s_sq, s + 1)
                    pool.nop(nofuse=True)
                    pool.partition_all_reduce(fro_now[:, u:u + 1], ssq[:, u:u + 1], P, RADD).then_inc(s_fro, 1)
                if is_step(s, 1, NT):
                    wait(pool, s_ve, s)
                    pool.nop(nofuse=True)
                    pool.tensor_tensor(rs2[:, 1 - u:2 - u], ve2[:, 1 - u:2 - u], minus_half[:, 0:1], ALU.pow).then_inc(s_rs, 1)

            graph_steps(pool, step)

            for u in range(2):
                pool.wait_ge(s_idst[u], 32 * (NT // 2))
            pool.wait_ge(s_blk, 1)
            pool.indirect_dma_start(out=ids[0:SLOT_TILES, :], out_offset=None, in_=idtab,
                                    in_offset=AT(ap=blk_i[0:SLOT_TILES, 0:1], axis=0)).then_inc(s_ids, 16)
            for u in range(2):
                pool.wait_ge(s_hst[u], 16 * (NT // 2))
                pool.wait_ge(s_x1st[u], 16 * (NT // 2))
            pool.wait_ge(s_table, 1)

            def gather(t, u):
                pool.tensor_copy(src_now[:, u:u + 1], tile_src[:, bass.ds(t, 1)]).then_inc(s_src, 1)
                wait(pool, s_src, t + 1)
                pool.nop(nofuse=True)
                pool.indirect_dma_start(out=xg[:, u], out_offset=None, in_=hrows,
                                        in_offset=AT(ap=src_now[:, u:u + 1], axis=0)).then_inc(s_xg[u], 16)

            def gather_next(t, u):
                wait(pool, s_wsel, t - 1)
                pool.nop(nofuse=True)
                wait(pool, s_xgT, t - 1)
                pool.nop(nofuse=True)
                gather(t, u)

            gather(0, 0)
            gather(1, 1)
            gather_next(2, 0)

            def scatter(t, u):
                pool.tensor_copy(dst_now[:, u:u + 1], tile_dst[:, bass.ds(t, 1)]).then_inc(s_dst, 1)
                wait(pool, s_dst, t + 1)
                pool.nop(nofuse=True)
                wait(pool, s_yg, t + 1)
                pool.nop(nofuse=True)
                wait(pool, s_add, 16 * t)
                pool.nop(nofuse=True)
                pool.indirect_dma_start(out=out, out_offset=AT(ap=dst_now[:, u:u + 1], axis=0),
                                        in_=yg[:, u], in_offset=None, bounds_check=N - 1, oob_is_err=False,
                                        compute_op=ALU.add).then_inc(s_add, 16)

            def step(t, u, k):
                if is_step(t, 0, SLOT_TILES - 4):
                    gather_next(t + 3, 1 - u)
                if is_step(t, 1, SLOT_TILES):
                    scatter(t - 1, 1 - u)

            slot_steps(pool, step, rounds=(SLOT_TILES - 7) // 4, end=SLOT_TILES + 1)
            pool.wait_ge(s_add, 16 * SLOT_TILES)

        @block.scalar
        def _(act):
            act.wait_ge(s_const, 6)
            for i, (src, dst) in enumerate(((bank[2], selfT), (bank[3], nbT))):
                act.wait_ge(s_setT, i + 1)
                act.activation(dst, src[:].rearrange("p (k d) -> p k d", k=KD), ACT.Copy).then_inc(s_setTc, 1)
            for i, (src, dst) in enumerate(((bank[4], ws_prod), (bank[5], wn_prod))):
                act.wait_ge(s_setP, i + 1)
                act.activation(dst[:], src[:].rearrange("p (k d) -> p k d", k=KD), ACT.Copy).then_inc(s_setPc, 1)
            for g in range(4):
                act.wait_ge(s_xn, g + 1)
                act.activation(XH[:, 4 * g:4 * g + 4, 0:D], x0[:, 4 * g:4 * g + 4], ACT.Copy).then_inc(s_xh, 1)

            def step(s, u, k):
                if is_step(s, 1, NT):
                    wait(act, s_agg, s)
                    wait(act, s_pre, s - 1)
                    act.activation(cT[:], agg_ps[1 - u][:].rearrange("p (k s) -> p k s", s=P), ACT.Copy).then_inc(s_ctc, 1)
                    hi, _ = wsplit(1 - u, bass.ds(k if u else k - 1, 1))
                    wait(act, s_scale, s)
                    act.activation(hi, stage_w(1 - u), ACT.Copy,
                                   scale=w_scale[:, bass.ds(s - 1, 1)].bitcast(F32)).then_inc(s_whi, 1)
                if is_step(s, 0, NT - 1):
                    junk, _ = wsplit(u, bass.ds(k, 1))
                    wait(act, s_w[u], 16 * (k + 1))
                    wait(act, s_frc, s - 1)
                    act.activation(junk, stage_w(u), ACT.Square, accum_out=ssq[:, u:u + 1]).then_inc(s_sq, 1)
                if is_step(s, 2, ROUTE_LAST):
                    wait(act, s_ht, s - 1)
                    wait(act, s_lg, s - 2)
                    act.activation(hT[:], hT_ps, ACT.Copy).then_inc(s_htc, 1)
                if is_step(s, 1, NT):
                    wait(act, s_pre, s)
                    wait(act, s_rdeg, s)
                    wait(act, s_prec, s - 1)
                    act.activation(mean_nb[:], pre_ps[:, 0:D], ACT.Copy, scale=rdeg[:, 1 - u:2 - u]).then_inc(s_nb, 1)
                if is_step(s, 2, ROUTE_LAST):
                    wait(act, s_shift, s - 1)
                    act.activation(pexp[:], lshift[:], ACT.Exp, accum_out=psum_e[:]).then_inc(s_pexp, 1)
                    wait(act, s_vdiff, s - 1)
                    act.activation(ediff[:], vdiff[:], ACT.Exp).then_inc(s_ediff, 1)

            graph_steps(act, step)

            act.wait_ge(s_param, 1)
            act.wait_ge(s_wlo, NT)
            act.wait_ge(s_table, 1)

            def step(t, u, k):
                e = act.value_load(tile_expert[0:1, bass.ds(t, 1)], min_val=0, max_val=E - 1)
                for half in range(2):
                    wait(act, s_mm1[half], t + 1)
                    wait(act, s_hidl[half], t)
                    for c in range(4 * half, 4 * half + 4):
                        src = bank[1 + 2 * u + half][:, (c % 4) * P:(c % 4 + 1) * P]
                        ins = act.activation(act32[:, c], src, ACT.Relu, scale=scaleA[:, bass.ds(e, 1)],
                                             bias=biasA[:, bass.ds(e, 1), c:c + 1].rearrange("p a c -> p (a c)"))
                    ins.then_inc(s_act[half], 1)

            slot_steps(act, step)

        @block.vector
        def _(dve):
            n = 0
            for g in range(4):
                dve.wait_ge(s_xin[g], 16)
                for t in range(4 * g, 4 * g + 4):
                    dve.bn_stats(ln_stat[:, t], x0[:, t]).then_inc(s_set, 1)
                    n += 1
            dve.wait_ge(s_set, n)
            for t in range(NT):
                dve.bn_aggr(ln_mv[:, t], ln_stat[:, t]).then_inc(s_set, 1)
                n += 1
            dve.wait_ge(s_set, n)
            dve.tensor_scalar(ln_ve[:], ln_mv[:, :, 1], EPS, None, ALU.add).then_inc(s_set, 1)
            n += 1
            dve.wait_ge(s_b1T, 1)
            dve.tensor_copy(bT[:], bank[7][:, 0:NB]).then_inc(s_b1q, 1)
            dve.wait_ge(s_b1q, 1)
            dve.wait_ge(s_const, 6)
            for i in range(2 * KD):
                dve.tensor_scalar(bias_cols[:, i], ones_b[:], bT[:, E * KI + i:E * KI + i + 1], None, ALU.mult).then_inc(s_bcols, 1)
            dve.wait_ge(s_rstd, 1)
            for g in range(5):
                if g < 4:
                    for t in range(4 * g, 4 * g + 4):
                        ins = dve.tensor_scalar(x0[:, t], x0[:, t], ln_mv[:, t, 0:1], ln_rs[:, t:t + 1], ALU.subtract, ALU.mult)
                        if t % 4 < 3:
                            ins.then_inc(s_set, 1)
                            n += 1
                    ins.then_inc(s_xn, 1)
                if g >= 1:
                    part = slice(4 * g - 4, 4 * g)
                    dve.wait_ge(s_set, n)
                    dve.wait_ge(s_xn, g)
                    dve.wait_ge(s_xh, g)
                    dve.tensor_tensor(XL[:, part], x0[:, part], XH[:, part, 0:D], ALU.subtract).then_inc(s_xl, 1)
            dve.wait_ge(s_setP, 3)
            dve.tensor_tensor(bias[:], bank[6][:, 0:D], bias[:], ALU.add).then_inc(s_bias, 1)
            dve.tensor_tensor(b1sq, bT[:, 0:E * KI], bT[:, 0:E * KI], ALU.mult).then_inc(s_set, 1)
            n += 1
            dve.wait_ge(s_set, n)
            dve.tensor_reduce(b1q[:], b1sq.rearrange("p (e c) -> p e c", e=E), AX, ALU.add).then_inc(s_b1q, 1)
            dve.wait_ge(s_bias, 1)

            GATE = 11
            SLOT = 3
            LN = 2

            def mask(s, u):
                for half in range(2):
                    wait(dve, s_tr[half], s + 1)
                    wait(dve, s_agg, s - 1)
                    dve.tensor_scalar(maskT[:, u, HJ * half:HJ * (half + 1)], mask_ps[half], 0.0, None,
                                      ALU.is_gt).then_inc(s_mask[half], 1)

            mask(0, 0)

            def step(s, u, k):
                o = 1 - u
                if is_step(s, 1, NT):
                    col = bass.ds(s - 1, 1)
                    wait(dve, s_fro, s)
                    dve.tensor_scalar(half_exp[:, col], fro_now[:, o:o + 1].bitcast(I32), 24, None, ALU.logical_shift_right).then_inc(s_scl, 1)
                    wait(dve, s_scl, s)
                    dve.tensor_scalar(w_scale[:, col], half_exp[:, col], -float(2 ** 23), float((189 + TOP_EXP) * 2 ** 23),
                                      ALU.mult, ALU.add).then_inc(s_scale, 1)
                    dve.tensor_copy(fro[:, col], fro_now[:, o:o + 1]).then_inc(s_frc, 1)
                if is_step(s, 2, ROUTE_LAST):
                    wait(dve, s_rs, s - 1)
                    wait(dve, s_ht, s - 2)
                    wait(dve, s_hlo, s - 2)
                    dve.tensor_scalar(h32[:], x1[:, u], mv2[:, u, 0:1], rs2[:, u:u + 1], ALU.subtract, ALU.mult).then_inc(s_h, 1)
                if is_step(s, 1, NT):
                    wait(dve, s_agg, s)
                    wait(dve, s_rank, s - 3)
                    wait(dve, s_nb, s - 2)
                    dve.tensor_scalar(deg[:, o:o + 1], deg_ps, 1.0, None, ALU.max).then_inc(s_deg, 1)
                    wait(dve, s_deg, s)
                    dve.reciprocal(rdeg[:, o:o + 1], deg[:, o:o + 1]).then_inc(s_rdeg, 1)
                if is_step(s, 4, LAST):
                    r, base = s - 4, (s - 4) * SLOT
                    wait(dve, s_rank, r + 1)
                    dve.tensor_tensor(place[:], rank_ps, expert_base[:], ALU.add).then_inc(s_slot, 1)
                    dve.tensor_tensor(chosen_sum[:], chosen_sum[:], chosen[:, u], ALU.add).then_inc(s_slot, 1)
                    wait(dve, s_slot, base + 1)
                    for c in range(2):
                        ins = dve.tensor_tensor_reduce(pjunk[:, c], place[:], pick[:, u, c], 1.0, 0.0, ALU.mult, ALU.add, dest[:, c:c + 1])
                    ins.then_inc(s_slot, 1)
                    wait(dve, s_slot, base + 3)
                    wait(dve, s_idst[u], 32 * (k - 2))
                    dve.tensor_copy(dest_i[:, u], dest[:]).then_inc(s_dest, 1)
                if is_step(s, 0, NT - 2):
                    mask(s + 1, o)
                if is_step(s, 1, NT):
                    hi, lo = wsplit(o, bass.ds(k if u else k - 1, 1))
                    wait(dve, s_whi, s)
                    dve.scalar_tensor_tensor(out=lo, in0=stage_w(o),
                                             scalar=w_scale[:, bass.ds(s - 1, 1)].bitcast(F32),
                                             in1=hi,
                                             op0=ALU.mult, op1=ALU.subtract).then_inc(s_wlo, 1)
                    c, base = s - 1, (s - 1) * LN
                    wait(dve, s_nb, c + 1)
                    dve.tensor_tensor(pre[:], mean_nb[:], pre_ps[:, D:2 * D], ALU.add).then_inc(s_prec, 1)
                    wait(dve, s_prec, c + 1)
                    wait(dve, s_x[o], 16 * (k + u))
                    dve.scalar_tensor_tensor(out=x1[:, o], in0=pre[:], scalar=0.0, in1=x1[:, o],
                                             op0=ALU.max, op1=ALU.add).then_inc(s_x1, 1)
                    wait(dve, s_x1, c + 1)
                    dve.bn_stats(st2[:], x1[:, o]).then_inc(s_ln, 1)
                    wait(dve, s_ln, base + 1)
                    dve.nop(nofuse=True)
                    dve.bn_aggr(mv2[:, o], st2[:]).then_inc(s_ln, 1)
                    wait(dve, s_ln, base + 2)
                    dve.tensor_scalar(ve2[:, o:o + 1], mv2[:, o, 1:2], EPS, None, ALU.add).then_inc(s_ve, 1)
                if is_step(s, 2, ROUTE_LAST):
                    r = s - 2
                    base = r * GATE
                    wait(dve, s_lg, r + 1)
                    dve.tensor_tensor(lg[:], lg_ps, gb[:], ALU.add).then_inc(s_lgc, 1)
                    wait(dve, s_lgc, r + 1)
                    dve.tensor_reduce(lmax[:], lg[:], AX, ALU.max).then_inc(s_gate, 1)
                    wait(dve, s_gate, base + 1)
                    dve.tensor_scalar(lshift[:], lg[:], lmax[:], None, ALU.subtract).then_inc(s_shift, 1)
                    wait(dve, s_pexp, r + 1)
                    dve.reciprocal(prec[:], psum_e[:]).then_inc(s_gate, 1)
                    wait(dve, s_gate, base + 2)
                    dve.tensor_scalar(prob[:], pexp[:], prec[:], None, ALU.mult).then_inc(s_gate, 1)
                    wait(dve, s_gate, base + 3)
                    dve.nop(nofuse=True)
                    dve.max(top[:], prob[:]).then_inc(s_gate, 1)
                    wait(dve, s_gate, base + 4)
                    dve.tensor_tensor(vdiff[:], top[:, 1:2], top[:, 0:1], ALU.subtract).then_inc(s_vdiff, 1)
                    dve.max_index(top_i[:], top[:], prob[:]).then_inc(s_gate, 1)
                    wait(dve, s_gate, base + 5)
                    dve.tensor_copy(top_f[:], top_i[:, 0:2]).then_inc(s_gate, 1)
                    wait(dve, s_gate, base + 6)
                    for c in range(2):
                        dve.tensor_scalar(pick[:, u, c], iota_e[:], top_f[:, c:c + 1], None, ALU.is_equal).then_inc(s_gate, 1)
                    wait(dve, s_gate, base + 8)
                    wait(dve, s_rank, r - 1)
                    dve.tensor_tensor(chosen[:, u], pick[:, u, 0], pick[:, u, 1], ALU.add).then_inc(s_chosen, 1)
                    wait(dve, s_ediff, r + 1)
                    dve.tensor_scalar(eplus[:], ediff[:], 1.0, None, ALU.add).then_inc(s_gate, 1)
                    wait(dve, s_gate, base + 9)
                    dve.reciprocal(gate0[:], eplus[:]).then_inc(s_gate, 1)
                    wait(dve, s_gate, base + 10)
                    wait(dve, s_hst[u], 16 * (k - 1))
                    meta = hrow[:, u, D:ROW]
                    dve.tensor_copy(meta[:, 0:1], gate0[:]).then_inc(s_gate, 1)
                    dve.scalar_tensor_tensor(out=meta[:, 1:2], in0=ediff[:], scalar=-1.0, in1=gate0[:],
                                             op0=ALU.add, op1=ALU.mult).then_inc(s_meta, 1)

            graph_steps(dve, step)

            dve.wait_ge(s_cnt, 1)
            n = 0

            def link(ins):
                nonlocal n
                ins.then_inc(s_tab, 1)
                n += 1
                dve.wait_ge(s_tab, n)

            link(dve.tensor_copy(cnt[:], cnt_ps))
            link(dve.tensor_scalar(cnt_i[:], cnt[:], float(P - 1), None, ALU.add))
            link(dve.tensor_scalar(tiles_i[:], cnt_i[:], 7, None, ALU.logical_shift_right))
            link(dve.tensor_copy(ntile[:], tiles_i[:]))
            src = ntile[:]
            for i, d in enumerate((1, 2, 4)):
                link(dve.tensor_copy(pfx[:, i, 0:d], src[:, 0:d]))
                link(dve.tensor_tensor(pfx[:, i, d:E], src[:, d:E], src[:, 0:E - d], ALU.add))
                src = pfx[:, i]
            link(dve.tensor_tensor(start_t[:], src, ntile[:], ALU.subtract))
            link(dve.tensor_scalar(past[:], src, iota_p[:], None, ALU.is_le))
            link(dve.scalar_tensor_tensor(out=owns[:], in0=start_t[:], scalar=iota_p[:], in1=past[:], op0=ALU.is_le, op1=ALU.subtract))
            link(dve.tensor_scalar(local[:], start_t[:], iota_p[:], -1.0, ALU.subtract, ALU.mult))
            link(dve.tensor_tensor(blk[:], local[:], expert_blk[:], ALU.add))
            link(dve.scalar_tensor_tensor(out=left[:], in0=local[:], scalar=-float(P), in1=cnt[:], op0=ALU.mult, op1=ALU.add))
            for i, t in enumerate((blk, left, iota_e)):
                link(dve.tensor_tensor_reduce(tjunk[:, i], t[:], owns[:], 1.0, 0.0, ALU.mult, ALU.add, tcol[:, i:i + 1]))
            dve.tensor_copy(blk_i[:], tcol[:, 0:1]).then_inc(s_blk, 1)

            dve.wait_ge(s_b1f, 1)
            m = 0

            def plink(ins):
                nonlocal m
                ins.then_inc(s_prm, 1)
                m += 1
                dve.wait_ge(s_prm, m)

            step_bits = float(2 ** 23)
            by_tensor = "p (e u) -> p e u"
            plink(dve.tensor_scalar(w_inv[:], half_exp[:], step_bits, float((65 - TOP_EXP) * 2 ** 23), ALU.mult, ALU.add))
            plink(dve.tensor_scalar(hq[:], b1fro[:], 2.0, None, ALU.mult))
            plink(dve.scalar_tensor_tensor(out=hq[:], in0=fro[:].rearrange(by_tensor, u=2)[:, :, 0], scalar=2.0 * D, in1=hq[:],
                                           op0=ALU.mult, op1=ALU.add))
            plink(dve.tensor_scalar(h_half[:], hq[:].bitcast(I32), 24, None, ALU.logical_shift_right))
            plink(dve.tensor_scalar(h_scale[:], h_half[:], -step_bits, float((189 + TOP_EXP) * 2 ** 23), ALU.mult, ALU.add))
            plink(dve.tensor_scalar(h_inv[:], h_half[:], step_bits, float((65 - TOP_EXP) * 2 ** 23), ALU.mult, ALU.add))
            inv = w_inv[:].bitcast(F32).rearrange(by_tensor, u=2)
            plink(dve.tensor_tensor(scaleA[:], h_scale[:].bitcast(F32), inv[:, :, 0], ALU.mult))
            plink(dve.tensor_tensor(scaleY[:], h_inv[:].bitcast(F32), inv[:, :, 1], ALU.mult))
            hs = h_scale[:].bitcast(F32)
            dve.tensor_tensor(biasA[:], b1T, hs.unsqueeze(2).to_broadcast([P, E, KI]), ALU.mult).then_inc(s_param, 1)

            dve.wait_ge(s_ids, 16)
            R = SLOT_TILES
            link(dve.tensor_scalar(tok_i[0:R, 0], ids[0:R, :], 1, None, ALU.logical_shift_right))
            link(dve.tensor_scalar(tok_i[0:R, 1], ids[0:R, :], 1, None, ALU.bitwise_and))
            link(dve.tensor_copy(tok_f[0:R, 0], tok_i[0:R, 0]))
            link(dve.tensor_copy(tok_f[0:R, 2], tok_i[0:R, 1]))
            link(dve.tensor_scalar(beyond[0:R, :], iota_f[0:R, :], tcol[0:R, 1:2], 2.0 * N, ALU.is_ge, ALU.mult))
            dve.tensor_tensor(tok_f[0:R, 1], tok_f[0:R, 0], beyond[0:R, :], ALU.add).then_inc(s_tokf, 1)
            dve.wait_ge(s_tabT, 1)
            link(dve.tensor_copy(tile_src[:], bank[4][:, 0:R]))
            link(dve.tensor_copy(tile_dst[:], bank[4][:, 64:64 + R]))
            link(dve.tensor_copy(tile_choice[:], bank[4][:, 128:128 + R]))
            dve.tensor_copy(tile_expert[:], bank[4][0:1, 192:192 + R]).then_inc(s_table, 1)
            dve.wait_ge(s_table, 1)
            dve.wait_ge(s_b2, 16)

            def rows_turned(t, u):
                wait(dve, s_xgT, t + 1)
                wait(dve, s_mm1[1], t - 1)
                dve.tensor_copy(xgT[:, u], bank[0][:, 0:2 * P].bitcast(F16).rearrange("p (j s) -> p j s", s=P)).then_inc(s_xgc, 1)
                meta = xg[:, u, D:ROW]
                dve.scalar_tensor_tensor(out=gate[:, bass.ds(t, 1)], in0=meta[:, 1:2], scalar=tile_choice[:, bass.ds(t, 1)],
                                         in1=meta[:, 0:1], op0=ALU.mult, op1=ALU.add).then_inc(s_wsel, 1)

            def rows_out(t, u):
                e = dve.value_load(tile_expert[0:1, bass.ds(t, 1)], min_val=0, max_val=E - 1)
                wait(dve, s_mm2, t + 1)
                wait(dve, s_yg, t)
                dve.scalar_tensor_tensor(out=y32, in0=bank[5 + u][:, D:2 * D], scalar=scaleY[:, bass.ds(e, 1)],
                                         in1=b2_all[:, bass.ds(e, 1)].rearrange("p a d -> p (a d)"),
                                         op0=ALU.mult, op1=ALU.add).then_inc(s_ylo, 1)
                wait(dve, s_ylo, t + 1)
                dve.scalar_tensor_tensor(out=y32, in0=bank[5 + u][:, 0:D], scalar=scaleY[:, bass.ds(e, 1)],
                                         in1=y32, op0=ALU.mult, op1=ALU.add).then_inc(s_y32, 1)
                wait(dve, s_y32, t + 1)
                wait(dve, s_wsel, t + 1)
                if not isinstance(t, int) or t >= 2:
                    wait(dve, s_add, (t - 1) * 16)
                dve.tensor_scalar(yg[:, u], y32, gate[:, bass.ds(t, 1)], None, ALU.mult).then_inc(s_yg, 1)

            rows_turned(0, 0)

            def step(t, u, k):
                for half in range(2):
                    part = slice(4 * half, 4 * half + 4)
                    wait(dve, s_act[half], t + 1)
                    wait(dve, s_mm2, t - 1)
                    dve.tensor_copy(hid_h[:, u, part], act32[:, part]).then_inc(s_hidh[half], 1)
                    wait(dve, s_hidh[half], t + 1)
                    dve.tensor_tensor(hid_l[:, u, part], act32[:, part], hid_h[:, u, part], ALU.subtract).then_inc(s_hidl[half], 1)
                    if half == 0 and is_step(t, 0, SLOT_TILES - 2):
                        rows_turned(t + 1, 1 - u)
                if not isinstance(t, int) or t >= 1:
                    rows_out(t - 1, 1 - u)

            slot_steps(dve, step)
            rows_out(SLOT_TILES - 1, 0)

        @block.tensor
        def _(pe):
            pe.wait_ge(s_const, 14)
            pe.wait_ge(s_small, 96)
            pe.transpose(bank[7][:, 0:NB], b_rows, ident_f[0:NB, 0:NB]).then_inc(s_b1T, 1)
            pe.wait_ge(s_wself, 32)
            for src, dst in ((raw_self, bank[2]), (raw_nb, bank[3])):
                for kb in range(KD):
                    for ka in range(KD):
                        at = kb * D + ka * P
                        ins = pe.transpose(dst[:, at:at + P], src[:, ka, kb * P:(kb + 1) * P], ident_f[:])
                ins.then_inc(s_setT, 1)
            pe.wait_ge(s_wcomb, 16)
            for i, (src, dst) in enumerate(((selfT, bank[4]), (nbT, bank[5]))):
                pe.wait_ge(s_setTc, i + 1)
                for ka in range(KD):
                    for kb in range(KD):
                        ins = pe.matmul(dst[:, ka * D:(ka + 1) * D], src[:, kb, ka * P:(ka + 1) * P], raw_comb[:, i * KD + kb],
                                        start=(kb == 0), stop=(kb == KD - 1))
                ins.then_inc(s_setP, 1)
            pe.wait_ge(s_bcols, 2 * KD)
            for i in range(2 * KD):
                ins = pe.matmul(bank[6][:, 0:D], bias_cols[:, i], raw_comb[:, i], start=(i == 0), stop=(i == 2 * KD - 1))
            ins.then_inc(s_setP, 1)
            pe.wait_ge(s_setPc, 2)
            pe.wait_ge(s_bias, 1)
            pe.wait_ge(s_b1q, 1)

            def transpose_rows(s, u, k):
                wait(pe, s_adj[u], 16 * (k + 1))
                for half in range(2):
                    wait(pe, s_mask[half], s)
                    for j in range(HJ):
                        at = (half * HJ + j) * P
                        ins = pe.transpose(mask_ps[half][:, j], adj_rows[:, u, at:at + P], ident_b[:])
                    ins.then_inc(s_tr[half], 1)

            def aggregate(s, u, half):
                for j in range(HJ * half, HJ * (half + 1)):
                    if isinstance(s, int) and s == 0 and j % 4 == 0:
                        pe.wait_ge(s_xl, j // 4 + 1)
                    for kd in range(KD):
                        cols = slice(kd * P, (kd + 1) * P)
                        pe.matmul(agg_ps[u][:, cols], XH[:, j, cols], maskT[:, u, j], start=(j == 0 and kd == 0), stop=False)
                        pe.matmul(agg_ps[u][:, cols], XL[:, j, cols], maskT[:, u, j], start=False, stop=(j == NT - 1 and kd == KD - 1))

            transpose_rows(0, 0, 0)

            def step(s, u, k):
                if is_step(s, 0, NT - 1):
                    wait(pe, s_mask[0], s + 1)
                    wait(pe, s_ctc, s - 1)
                    aggregate(s, u, 0)
                if is_step(s, 0, NT - 2):
                    transpose_rows(s + 1, 1 - u, k + u)
                if is_step(s, 0, NT - 1):
                    wait(pe, s_mask[1], s + 1)
                    aggregate(s, u, 1)
                    for kd in range(KD):
                        cols = slice(kd * P, (kd + 1) * P)
                        dst = agg_ps[u][:, D + kd * P:D + (kd + 1) * P]
                        pe.matmul(dst, XH[:, bass.ds(s, 1), cols].rearrange("p a d -> p (a d)"), ident_h[:], start=True, stop=False)
                        ins = pe.matmul(dst, XL[:, bass.ds(s, 1), cols].rearrange("p a d -> p (a d)"), ident_h[:], start=False, stop=True)
                    wait(pe, s_rdeg, s)
                    wait(pe, s_dest, s - 3)
                    for j in range(NT):
                        ins = pe.matmul(deg_ps, maskT[:, u, j], XH[:, j, D:D + 1], start=(j == 0), stop=(j == NT - 1))
                    ins.then_inc(s_agg, 1)
                if is_step(s, 3, RANK_LAST):
                    wait(pe, s_chosen, s - 2)
                    wait(pe, s_dest, s - 3)
                    pe.matmul(rank_ps, before[:], chosen[:, 1 - u], start=True, stop=False)
                    pe.matmul(rank_ps, ones_b[:], chosen_sum[:], start=False, stop=True).then_inc(s_rank, 1)
                if is_step(s, 2, ROUTE_LAST):
                    wait(pe, s_h, s - 1)
                    wait(pe, s_htc, s - 2)
                    for kd in range(KD):
                        ins = pe.transpose(hT_ps[:, kd], h32[:, kd * P:(kd + 1) * P], ident_f[:])
                    ins.then_inc(s_ht, 1)
                if is_step(s, 1, NT):
                    wait(pe, s_ctc, s)
                    wait(pe, s_prec, s - 1)
                    for kd in range(KD):
                        pe.matmul(pre_ps[:, 0:D], cT[:, kd], wn_prod[:, kd], start=(kd == 0), stop=(kd == KD - 1))
                    for kd in range(KD):
                        pe.matmul(pre_ps[:, D:2 * D], cT[:, KD + kd], ws_prod[:, kd], start=(kd == 0), stop=False)
                    pe.matmul(pre_ps[:, D:2 * D], ident_f[:], bias[:], start=False, stop=True).then_inc(s_pre, 1)
                if is_step(s, 2, ROUTE_LAST):
                    wait(pe, s_htc, s - 1)
                    wait(pe, s_lgc, s - 2)
                    for kd in range(KD):
                        ins = pe.matmul(lg_ps, hT[:, kd], gw[:, kd], start=(kd == 0), stop=(kd == KD - 1))
                    ins.then_inc(s_lg, 1)

            graph_steps(pe, step)

            pe.wait_ge(s_dest, NT)
            pe.matmul(cnt_ps, ones_b[:], chosen_sum[:], start=True, stop=True).then_inc(s_cnt, 1)
            pe.wait_ge(s_tokf, 1)
            R = SLOT_TILES
            for i in range(3):
                pe.transpose(bank[4][:, 64 * i:64 * i + R], tok_f[0:R, i], ident_f[0:R, 0:R])
            pe.transpose(bank[4][0:1, 192:192 + R], tcol[0:R, 2:3], ident_f[0:R, 0:R]).then_inc(s_tabT, 1)

            def turn_rows(t, u, k):
                wait(pe, s_xg[u], 16 * (k + 1))
                wait(pe, s_xgc, t)
                for j in range(4):
                    ins = pe.transpose(bank[0][:, 64 * j:64 * (j + 1)].bitcast(F16), xg[:, u, j * 64:(j + 1) * 64].bitcast(F16), ident_h[:])
                ins.then_inc(s_xgT, 1)

            def expert_of(t):
                return pe.value_load(tile_expert[0:1, bass.ds(t, 1)], min_val=0, max_val=E - 1)

            def up(e, t, u, c):
                if c == 0:
                    wait(pe, s_xgc, t + 1)
                if c % 4 == 0:
                    wait(pe, s_act[c // 4], t - 1)
                dst = bank[1 + 2 * u + c // 4][:, (c % 4) * P:(c % 4 + 1) * P]
                for kd in range(KD):
                    cols = slice(c * P, (c + 1) * P)
                    hi = W1H[:, bass.ds(e, 1), kd, cols].rearrange("p a i -> p (a i)")
                    lo = W1L[:, bass.ds(e, 1), kd, cols].rearrange("p a i -> p (a i)")
                    pe.matmul(dst, hi, xgT[:, u, kd], start=(kd == 0), stop=False)
                    pe.matmul(dst, hi, xgT[:, u, KD + kd], start=False, stop=False)
                    ins = pe.matmul(dst, lo, xgT[:, u, kd], start=False, stop=(kd == KD - 1))
                if c % 4 == 3:
                    ins.then_inc(s_mm1[c // 4], 1)

            def down(e, t, u, c):
                if c == 0:
                    wait(pe, s_y32, t - 1)
                if c % 4 == 0:
                    wait(pe, s_hidl[c // 4], t + 1)
                both = W2S[:, bass.ds(e, 1), c].rearrange("p a d -> p (a d)")
                hi = W2S[:, bass.ds(e, 1), c, 0:D].rearrange("p a d -> p (a d)")
                pe.matmul(bank[5 + u][:], hid_h[:, u, c], both, start=(c == 0), stop=False)
                ins = pe.matmul(bank[5 + u][:, 0:D], hid_l[:, u, c], hi, start=False, stop=(c == KI - 1))
                if c == KI - 1:
                    ins.then_inc(s_mm2, 1)

            pe.wait_ge(s_wlo, NT)
            pe.wait_ge(s_table, 1)
            turn_rows(0, 0, 0)

            e_last = None

            def new_round():
                nonlocal e_last
                e_last = None

            def step(t, u, k):
                nonlocal e_last
                e_now = expert_of(t)
                if e_last is None and is_step(t, 1, SLOT_TILES):
                    e_last = expert_of(t - 1)
                for c in range(KI):
                    up(e_now, t, u, c)
                    if is_step(t, 1, SLOT_TILES):
                        down(e_last, t - 1, 1 - u, c)
                    if c == 3 and is_step(t, 0, SLOT_TILES - 2):
                        turn_rows(t + 1, 1 - u, k + u)
                e_last = e_now

            slot_steps(pe, step, new_round)
            for c in range(KI):
                down(e_last, SLOT_TILES - 1, 0, c)


_INS = ['x', 'adj', 'L0_gnn_W_self', 'L0_gnn_b_self', 'L0_gnn_W_nb', 'L0_gnn_b_nb', 'L0_gnn_W_comb', 'L0_gnn_b_comb',
        'L0_ffn_gate_w', 'L0_ffn_gate_b', 'L0_ffn_w1', 'L0_ffn_b1', 'L0_ffn_w2', 'L0_ffn_b2']
_OUTS = [((2048, 256), 'float32')]


def kernel(**inputs):
    import numpy as _np
    import concourse.bacc as _bacc
    from concourse import mybir as _mybir
    from concourse.bass_utils import run_bass_kernel_spmd as _run

    nc = _bacc.Bacc("TRN2", target_bir_lowering=False, num_devices=1)
    arrays, args = {}, []
    for name in _INS:
        a = _np.ascontiguousarray(inputs[name])
        arrays[f"in_{name}_dram"] = a
        args.append(nc.dram_tensor(f"in_{name}_dram", a.shape, _mybir.dt.from_np(a.dtype), kind="ExternalInput").ap())
    for i, (shape, dtype) in enumerate(_OUTS):
        dt = _mybir.dt.from_np(_np.dtype(dtype))
        args.append(nc.dram_tensor(f"out_{i}_dram", shape, dt, kind="ExternalOutput").ap())
    gnn_moe_kernel(nc, *args)
    r = _run(nc, [arrays], core_ids=[0])
    got = tuple(r.results[0][f"out_{i}_dram"] for i in range(len(_OUTS)))
    return got[0]
```

```python
from contextlib import ExitStack

import concourse.bass as bass
from concourse import mybir

F32 = mybir.dt.float32
F16 = mybir.dt.float16
BF16 = mybir.dt.bfloat16
I32 = mybir.dt.int32
U32 = mybir.dt.uint32
ALU = mybir.AluOpType
ACT = mybir.ActivationFunctionType
AX = mybir.AxisListType.X
RADD = bass.bass_isa.ReduceOp.add
AT = bass.IndirectOffsetOnAxis

P = 128
EPS = 1e-5
TOP_EXP = 15


def wait(eng, sem, value):
    if isinstance(value, int) and value <= 0:
        return
    eng.wait_ge(sem, value)


def gnn_moe_kernel(nc, x, adj, w_self, b_self, w_nb, b_nb, w_comb, b_comb,
                   gate_w, gate_b, w1, b1, w2, b2, out):
    N, D = x.shape
    E, _, I = w1.shape
    KD = D // P
    KI = I // P
    NT = N // P
    HJ = NT // 2
    SLOT_TILES = (2 * N + E * (P - 1)) // P
    BLOCKS = N // P
    ROW = D + 2
    assert NT == 2 * E and BLOCKS * E == P and KD == 2

    hrows = nc.dram_tensor("hrows", [N, ROW], F32, kind="Internal").ap()
    idtab = nc.dram_tensor("idtab", [P, P], I32, kind="Internal").ap()
    idtab_flat = idtab.rearrange("b (s a) -> (b s) a", a=1)

    with ExitStack() as ctx:
        def sb(name, shape, dt):
            return ctx.enter_context(nc.sbuf_tensor(name, shape, dt))

        def psum(name, shape, dt):
            return ctx.enter_context(nc.psum_tensor(name, shape, dt))

        def sem(name):
            return ctx.enter_context(nc.semaphore(name))

        W1H = sb("W1H", [P, E, KD, I], F16)
        W1L = sb("W1L", [P, E, KD, I], F16)
        W2S = sb("W2S", [P, E, KI, 2 * D], F16)
        XH = sb("XH", [P, NT, D + 2], F16)
        XL = sb("XL", [P, NT, D], F16)
        adj_rows = sb("adj_rows", [P, 2, N], BF16)
        w_stage = sb("w_stage", [P, 2, KD * I], F32)
        maskT = sb("maskT", [P, 2, NT, P], F16)

        scr1 = W1L[:, E // 2:E].rearrange("p e k i -> p (e k i)").bitcast(F32)
        scr2 = W2S[:, 3 * E // 4:E].rearrange("p e k i -> p (e k i)").bitcast(F32)
        x0 = scr2.rearrange("p (t d) -> p t d", d=D)
        raw_self = scr1[:, 0:512].rearrange("p (k d) -> p k d", k=KD)
        raw_nb = scr1[:, 512:1024].rearrange("p (k d) -> p k d", k=KD)
        raw_comb = scr1[:, 1024:2048].rearrange("p (k d) -> p k d", k=2 * KD)
        selfT = scr1[:, 2048:2560].rearrange("p (k d) -> p k d", k=KD)
        nbT = scr1[:, 2560:3072].rearrange("p (k d) -> p k d", k=KD)
        bias_cols = scr1[:, 3072:3584].rearrange("p (k m) -> p k m", k=2 * KD)
        NB = E * KI + 2 * KD
        b_rows = scr1[0:NB, 3584:3712]
        b1sq = scr1[:, 3776:3840]

        ws_prod = sb("ws_prod", [P, KD, D], F32)
        wn_prod = sb("wn_prod", [P, KD, D], F32)
        bias = sb("bias", [P, D], F32)
        gw = sb("gw", [P, KD, E], F32)
        gb = sb("gb", [P, E], F32)
        bT = sb("bT", [P, NB], F32)
        b1T = bT[:, 0:E * KI].rearrange("p (e c) -> p e c", e=E)
        ident_f = sb("ident_f", [P, P], F32)
        ident_b = sb("ident_b", [P, P], BF16)
        ident_h = sb("ident_h", [P, P], F16)
        before = sb("before", [P, P], BF16)
        ones_b = sb("ones_b", [P, P], BF16)
        iota_e = sb("iota_e", [P, E], F32)
        expert_base = sb("expert_base", [P, E], F32)
        iota_p = sb("iota_p", [P, 1], F32)
        iota_f = sb("iota_f", [P, P], F32)
        slot_ids = sb("slot_ids", [P, NT * 2], I32)
        zero_ids = sb("zero_ids", [P, P], I32)
        minus_half = sb("minus_half", [P, NT], F32)

        ln_stat = sb("ln_stat", [P, NT, 6], F32)
        ln_mv = sb("ln_mv", [P, NT, 2], F32)
        ln_ve = sb("ln_ve", [P, NT], F32)
        ln_rs = sb("ln_rs", [P, NT], F32)
        mean_nb = sb("mean_nb", [P, D], F32)
        cT = sb("cT", [P, 4, P], F32)
        pre = sb("pre", [P, D], F32)
        x1 = sb("x1", [P, 2, D], F32)
        h32 = sb("h32", [P, D], F32)
        hT = sb("hT", [P, KD, P], F32)
        hrow = sb("hrow", [P, 2, ROW], F32)
        deg = sb("deg", [P, 2], F32)
        rdeg = sb("rdeg", [P, 2], F32)
        st2 = sb("st2", [P, 6], F32)
        mv2 = sb("mv2", [P, 2, 2], F32)
        ve2 = sb("ve2", [P, 2], F32)
        rs2 = sb("rs2", [P, 2], F32)
        nmr2 = sb("nmr2", [P, 2], F32)
        lg = sb("lg", [P, E], F32)
        lmax = sb("lmax", [P, 1], F32)
        lshift = sb("lshift", [P, E], F32)
        pexp = sb("pexp", [P, E], F32)
        psum_e = sb("psum_e", [P, 1], F32)
        prec = sb("prec", [P, 1], F32)
        prob = sb("prob", [P, E], F32)
        top = sb("top", [P, 8], F32)
        top_i = sb("top_i", [P, 8], U32)
        top_f = sb("top_f", [P, 2], F32)
        vdiff = sb("vdiff", [P, 1], F32)
        ediff = sb("ediff", [P, 1], F32)
        eplus = sb("eplus", [P, 1], F32)
        gate0 = sb("gate0", [P, 1], F32)
        pick = sb("pick", [P, 2, 2, E], F32)
        chosen = sb("chosen", [P, 2, E], BF16)
        chosen_sum = sb("chosen_sum", [P, E], BF16)
        place = sb("place", [P, E], F32)
        pjunk = sb("pjunk", [P, 2, E], F32)
        dest = sb("dest", [P, 2], F32)
        dest_i = sb("dest_i", [P, 2, 2], I32)
        ssq = sb("ssq", [P, 2], F32)
        fro_now = sb("fro_now", [P, 2], F32)
        fro = sb("fro", [P, 2 * E], F32)
        half_exp = sb("half_exp", [P, 2 * E], I32)
        w_scale = sb("w_scale", [P, 2 * E], I32)
        w_inv = sb("w_inv", [P, 2 * E], I32)
        b1q = sb("b1q", [P, E], F32)
        b1fro = sb("b1fro", [P, E], F32)
        hq = sb("hq", [P, E], F32)
        h_half = sb("h_half", [P, E], I32)
        h_scale = sb("h_scale", [P, E], I32)
        h_inv = sb("h_inv", [P, E], I32)
        scaleA = sb("scaleA", [P, E], F32)
        biasA = sb("biasA", [P, E, KI], F32)
        scaleY = sb("scaleY", [P, E], F32)

        cnt = sb("cnt", [P, E], F32)
        cnt_i = sb("cnt_i", [P, E], I32)
        tiles_i = sb("tiles_i", [P, E], I32)
        ntile = sb("ntile", [P, E], F32)
        pfx = sb("pfx", [P, 3, E], F32)
        start_t = sb("start_t", [P, E], F32)
        past = sb("past", [P, E], F32)
        owns = sb("owns", [P, E], F32)
        local = sb("local", [P, E], F32)
        blk = sb("blk", [P, E], F32)
        left = sb("left", [P, E], F32)
        tjunk = sb("tjunk", [P, 3, E], F32)
        tcol = sb("tcol", [P, 3], F32)
        blk_i = sb("blk_i", [P, 1], I32)
        expert_blk = sb("expert_blk", [P, E], F32)
        ids = sb("ids", [P, P], I32)
        tok_i = sb("tok_i", [P, 2, P], I32)
        tok_f = sb("tok_f", [P, 3, P], F32)
        beyond = sb("beyond", [P, P], F32)
        tile_src = sb("tile_src", [P, SLOT_TILES], I32)
        tile_dst = sb("tile_dst", [P, SLOT_TILES], I32)
        ids_now = sb("ids_now", [P, 2, 2], I32)
        src_now = sb("src_now", [P, 2], I32)
        dst_now = sb("dst_now", [P, 2], I32)
        tile_choice = sb("tile_choice", [P, SLOT_TILES], F32)
        tile_expert = sb("tile_expert", [1, SLOT_TILES], I32)

        ws_flat = w_stage[:].rearrange("p u n -> p (u n)")
        act32 = ws_flat[:, 0:KI * P].rearrange("p (c s) -> p c s", c=KI)
        hid_h = ws_flat[:, 1024:2048].bitcast(F16).rearrange("p (b c s) -> p b c s", b=2, c=KI)
        hid_l = ws_flat[:, 2048:3072].bitcast(F16).rearrange("p (b c s) -> p b c s", b=2, c=KI)
        b2_all = adj_rows[:].rearrange("p u n -> p (u n)").bitcast(F32).rearrange("p (e d) -> p e d", e=E)
        XL_flat = XL[:].rearrange("p t d -> p (t d)")
        mt_flat = maskT[:].rearrange("p u j s -> p (u j s)")
        xg = mt_flat[:, 0:4 * ROW].bitcast(F32).rearrange("p (b d) -> p b d", b=2)
        xgT = mt_flat[:, 2080:3104].rearrange("p (b j s) -> p b j s", b=2, j=4)
        yg = XL_flat[:, 0:1024].bitcast(F32).rearrange("p (b d) -> p b d", b=2)
        y32 = XL_flat[:, 1024:1536].bitcast(F32)
        w1h_now = XH[:].rearrange("p t d -> p (t d)")[:, 0:2 * KD * I].rearrange("p (b k i) -> p b k i", b=2, k=KD)
        gate = sb("gate", [P, SLOT_TILES], F32)

        bank = [psum(f"bank{i}", [P, 512], F32) for i in range(8)]
        mask_ps = [bank[i][:].bitcast(BF16).rearrange("p (j s) -> p j s", s=P) for i in range(2)]
        agg_ps = [bank[2], bank[3]]
        deg_ps = bank[4][:, 0:1]
        pre_ps = bank[5]
        hT_ps = bank[6][:, 0:D].rearrange("p (k s) -> p k s", s=P)
        lg_ps = bank[7][:, 0:E]
        rank_ps = bank[7][:, 16:16 + E]
        cnt_ps = bank[7][:, 32:32 + E]

        s_xin = [sem(f"s_xin{g}") for g in range(4)]
        s_wself = sem("s_wself")
        s_wcomb = sem("s_wcomb")
        s_small = sem("s_small")
        s_const = sem("s_const")
        s_set = sem("s_set")
        s_stat = sem("s_stat")
        s_aggr = sem("s_aggr")
        s_lnv = sem("s_lnv")
        s_rstd = sem("s_rstd")
        s_xn = sem("s_xn")
        s_xh = sem("s_xh")
        s_xl = sem("s_xl")
        s_setT = sem("s_setT")
        s_setTc = sem("s_setTc")
        s_setP = sem("s_setP")
        s_setPc = sem("s_setPc")
        s_bcols = sem("s_bcols")
        s_bias = sem("s_bias")
        s_b1T = sem("s_b1T")
        s_b1s = sem("s_b1s")
        s_b1q = sem("s_b1q")
        s_b1f = sem("s_b1f")
        s_gps = sem("s_gps")
        s_idz = sem("s_idz")

        s_adj = [sem(f"s_adj{u}") for u in range(2)]
        s_w = [sem(f"s_w{u}") for u in range(2)]
        s_x = [sem(f"s_xrow{u}") for u in range(2)]
        s_x1st = [sem(f"s_x1st{u}") for u in range(2)]
        s_hst = [sem(f"s_hst{u}") for u in range(2)]
        s_idst = [sem(f"s_idst{u}") for u in range(2)]
        s_tr = [sem("s_trA"), sem("s_trB")]
        s_mask = [sem("s_maskA"), sem("s_maskB")]
        s_agg = sem("s_agg")
        s_deg = sem("s_deg")
        s_rdeg = sem("s_rdeg")
        s_nb = sem("s_nb")
        s_ctc = sem("s_ctc")
        s_pre = sem("s_pre")
        s_prec = sem("s_prec")
        s_x1 = sem("s_x1")
        s_ln = sem("s_ln")
        s_ve = sem("s_ve")
        s_pow = sem("s_pow")
        s_rs = sem("s_rs")
        s_h = sem("s_h")
        s_ht = sem("s_ht")
        s_htc = sem("s_htc")
        s_lg = sem("s_lg")
        s_lgc = sem("s_lgc")
        s_slot = sem("s_slot")
        s_gate = sem("s_gate")
        s_shift = sem("s_shift")
        s_pexp = sem("s_pexp")
        s_vdiff = sem("s_vdiff")
        s_ediff = sem("s_ediff")
        s_meta = sem("s_meta")
        s_chosen = sem("s_chosen")
        s_rank = sem("s_rank")
        s_dest = sem("s_dest")
        s_hlo = sem("s_hlo")
        s_hhi = sem("s_hhi")
        s_sq = sem("s_sq")
        s_fro = sem("s_fro")
        s_scl = sem("s_scl")
        s_frc = sem("s_frc")
        s_scale = sem("s_scale")
        s_whi = sem("s_whi")
        s_wlo = sem("s_wlo")

        s_cnt = sem("s_cnt")
        s_tab = sem("s_tab")
        s_blk = sem("s_blk")
        s_ids = sem("s_ids")
        s_tok = sem("s_tok")
        s_tokf = sem("s_tokf")
        s_tabT = sem("s_tabT")
        s_table = sem("s_table")
        s_prm = sem("s_prm")
        s_param = sem("s_param")
        s_b2 = sem("s_b2")

        s_xg = [sem(f"s_xg{u}") for u in range(2)]
        s_src = sem("s_src")
        s_idn = sem("s_idn")
        s_dst = sem("s_dst")
        s_xgT = sem("s_xgT")
        s_xgc = sem("s_xgc")
        s_wsel = sem("s_wsel")
        s_wnow = [sem(f"s_wnow{u}") for u in range(2)]
        s_mm1 = [sem("s_mm1A"), sem("s_mm1B")]
        s_act = [sem("s_actA"), sem("s_actB")]
        s_hidh = [sem("s_hidhA"), sem("s_hidhB")]
        s_hidl = [sem("s_hidlA"), sem("s_hidlB")]
        s_mm2 = sem("s_mm2")
        s_ylo = sem("s_ylo")
        s_y32 = sem("s_y32")
        s_yg = sem("s_yg")
        s_add = sem("s_add")

        x_t = x.rearrange("(t p) d -> t p d", p=P)
        out_t = out.rearrange("(t p) d -> t p d", p=P)
        adj_t = adj.rearrange("(t p) j -> t p j", p=P)
        hrows_t = hrows.rearrange("(t p) d -> t p d", p=P)
        w1_t = w1.rearrange("e (k p) i -> e p k i", p=P)
        w2_t = w2.rearrange("e (c p) d -> e p c d", p=P)

        def stage_w(u):
            return w_stage[:, u].rearrange("p (k i) -> p k i", k=KD if u == 0 else KI)

        def wsplit(u, e):
            if u == 0:
                hi, lo = W1H[:, e], W1L[:, e]
            else:
                hi, lo = W2S[:, e, :, 0:D], W2S[:, e, :, D:2 * D]
            return hi.rearrange("p a k i -> p (a k) i"), lo.rearrange("p a k i -> p (a k) i")

        ROUTE_LAST = NT + 1
        SLOT_LAST = NT + 2
        LAST = NT + 3

        def graph_steps(eng, step):
            for s in range(6):
                step(s, s % 2, s // 2)
            with eng.Fori(0, NT // 2 - 5) as q:
                for u in range(2):
                    step(q * 2 + (6 + u), u, q + 3)
            for s in range(NT - 4, LAST + 1):
                step(s, s % 2, s // 2)

        def is_step(s, lo, hi):
            return not isinstance(s, int) or lo <= s <= hi

        def slot_steps(eng, step, new_round=None, per_round=4, spare=0, end=SLOT_TILES):
            rounds = (SLOT_TILES - 2 - spare) // per_round
            step(0, 0, 0)
            step(1, 1, 0)
            with eng.Fori(0, rounds) as q:
                if new_round:
                    new_round()
                for j in range(per_round):
                    step(q * per_round + (2 + j), j % 2, q * (per_round // 2) + (1 + j // 2), j == per_round - 1)
            if new_round:
                new_round()
            for t in range(2 + per_round * rounds, end):
                step(t, t % 2, t // 2)

        block = ctx.enter_context(nc.Block())

        @block.sync
        def _(sp):
            for g in range(4):
                sp.dma_start(x0[:, 4 * g:4 * g + 4], x_t[4 * g:4 * g + 4].rearrange("t p d -> p t d")).then_inc(s_xin[g], 16)
            sp.dma_start(raw_self, w_self.rearrange("(k p) d -> p k d", p=P)).then_inc(s_wself, 16)
            sp.dma_start(raw_nb, w_nb.rearrange("(k p) d -> p k d", p=P)).then_inc(s_wself, 16)
            sp.dma_start(raw_comb, w_comb.rearrange("(k p) d -> p k d", p=P)).then_inc(s_wcomb, 16)
            sp.dma_start(b_rows[E * KI:E * KI + KD, :], b_self.rearrange("(k p) -> k p", p=P)).then_inc(s_small, 16)
            sp.dma_start(b_rows[E * KI + KD:NB, :], b_nb.rearrange("(k p) -> k p", p=P)).then_inc(s_small, 16)
            sp.dma_start(bias[:], b_comb.partition_broadcast(P)).then_inc(s_small, 16)
            sp.dma_start(gw[:], gate_w.rearrange("(k p) e -> p k e", p=P)).then_inc(s_small, 16)
            sp.dma_start(gb[:], gate_b.partition_broadcast(P)).then_inc(s_small, 16)
            sp.dma_start(b_rows[0:E * KI, :], b1.rearrange("e (c p) -> (e c) p", p=P)).then_inc(s_small, 16)

            def load_w(i, u, k):
                src = w1_t if u == 0 else w2_t
                e = k
                sp.dma_start(stage_w(u), src[bass.ds(e, 1)].rearrange("a p k i -> p (a k) i")).then_inc(s_w[u], 16)

            load_w(0, 0, 0)
            load_w(1, 1, 0)

            def step(s, u, k):
                if is_step(s, 0, NT - 1):
                    wait(sp, s_h, s - 1)
                    wait(sp, s_x1st[u], 16 * k)
                    sp.dma_start(x1[:, u], x_t[bass.ds(s, 1)].rearrange("t p d -> p (t d)")).then_inc(s_x[u], 16)
                if isinstance(s, int) and s == NT - 1:
                    sp.wait_ge(s_tr[1], NT)
                    sp.dma_start(b2_all, b2.rearrange("e d -> (e d)").partition_broadcast(P).rearrange("p (e d) -> p e d", e=E)).then_inc(s_b2, 16)
                if is_step(s, 1, NT):
                    wait(sp, s_x1, s)
                    sp.dma_start(out_t[bass.ds(s - 1, 1)].rearrange("t p d -> p (t d)"), x1[:, 1 - u]).then_inc(s_x1st[1 - u], 16)
                if is_step(s, 1, NT - 2):
                    wait(sp, s_wlo, s)
                    load_w(s + 1, 1 - u, k + u)
                if is_step(s, 2, ROUTE_LAST):
                    wait(sp, s_hlo, s - 1)
                    wait(sp, s_meta, s - 1)
                    sp.dma_start(hrows_t[bass.ds(s - 2, 1)].rearrange("t p d -> p (t d)"), hrow[:, u]).then_inc(s_hst[u], 16)

            graph_steps(sp, step)

            sp.wait_ge(s_whi, NT)
            sp.wait_ge(s_agg, NT)
            sp.wait_ge(s_table, 1)

            def step(t, u, k, last_of_round=False):
                e = sp.value_load(tile_expert[0:1, bass.ds(t, 1)], min_val=0, max_val=E - 1)
                wait(sp, s_mm1[1], t - 1)
                sp.dma_start(w1h_now[:, u], W1H[:, bass.ds(e, 1)].rearrange("p a k i -> p (a k) i")).then_inc(s_wnow[u], 16)

            slot_steps(sp, step)

        @block.gpsimd
        def _(pool):
            for t in (ident_f, ident_b, ident_h):
                pool.memset(t[:], 0.0).then_inc(s_gps, 1)
            pool.memset(before[:], 1.0).then_inc(s_gps, 1)
            pool.memset(zero_ids[:], 0).then_inc(s_gps, 1)
            pool.wait_ge(s_gps, 5)
            pool.dma_start(idtab, zero_ids[:]).then_inc(s_idz, 16)

            def load_adj(s, u):
                pool.dma_start(adj_rows[:, u], adj_t[bass.ds(s, 1)].rearrange("t p j -> p (t j)")).then_inc(s_adj[u], 16)

            load_adj(0, 0)
            load_adj(1, 1)
            for t in (ident_f, ident_b, ident_h):
                pool.affine_select(out=t[:], in_=t[:], compare_op=ALU.not_equal, fill=1.0, base=0,
                                   pattern=[[-1, P]], channel_multiplier=1).then_inc(s_const, 1)
            pool.affine_select(out=before[:], in_=before[:], compare_op=ALU.is_gt, fill=0.0, base=0,
                               pattern=[[1, P]], channel_multiplier=-1).then_inc(s_const, 1)
            pool.memset(ones_b[:], 1.0).then_inc(s_const, 1)
            pool.memset(XH[:, :, D:D + 2], 1.0).then_inc(s_const, 1)
            pool.memset(chosen_sum[:], 0.0).then_inc(s_const, 1)
            pool.memset(minus_half[:], -0.5).then_inc(s_const, 1)
            pool.iota(iota_e[:], pattern=[[1, E]], base=0, channel_multiplier=0, allow_small_or_imprecise_dtypes=True).then_inc(s_const, 1)
            pool.iota(expert_base[:], pattern=[[N, E]], base=0, channel_multiplier=0, allow_small_or_imprecise_dtypes=True).then_inc(s_const, 1)
            pool.iota(expert_blk[:], pattern=[[BLOCKS, E]], base=0, channel_multiplier=0, allow_small_or_imprecise_dtypes=True).then_inc(s_const, 1)
            pool.iota(iota_p[:], pattern=[[0, 1]], base=0, channel_multiplier=1, allow_small_or_imprecise_dtypes=True).then_inc(s_const, 1)
            pool.iota(iota_f[:], pattern=[[1, P]], base=0, channel_multiplier=0, allow_small_or_imprecise_dtypes=True).then_inc(s_const, 1)
            pool.iota(slot_ids[:].rearrange("p (t c) -> p t c", c=2), pattern=[[2 * P, NT], [1, 2]], base=0, channel_multiplier=2).then_inc(s_const, 1)
            pool.wait_ge(s_const, 14)
            for g in range(4):
                part = slice(4 * g, 4 * g + 4)
                pool.wait_ge(s_lnv, g + 1)
                pool.tensor_tensor(ln_rs[:, part], ln_ve[:, part], minus_half[:, part], ALU.pow).then_inc(s_rstd, 1)
            pool.wait_ge(s_idz, 16)

            pool.wait_ge(s_tr[1], 1)
            load_adj(2, 0)
            pool.wait_ge(s_b1q, 2)
            pool.partition_all_reduce(b1fro[:], b1q[:], P, RADD).then_inc(s_b1f, 1)

            def weight_norm(s, u):
                wait(pool, s_sq, s + 1)
                pool.nop(nofuse=True)
                pool.partition_all_reduce(fro_now[:, u:u + 1], ssq[:, u:u + 1], P, RADD).then_inc(s_fro, 1)

            def step(s, u, k):
                if is_step(s, 4, LAST):
                    wait(pool, s_idst[u], 32 * (k - 2))
                    pool.nop(nofuse=True)
                    pool.tensor_copy(ids_now[:, u], slot_ids[:, bass.ds((s - 4) * 2, 2)]).then_inc(s_idn, 1)
                    wait(pool, s_idn, s - 3)
                    pool.nop(nofuse=True)
                    wait(pool, s_dest, s - 3)
                    pool.nop(nofuse=True)
                    for c in range(2):
                        pool.indirect_dma_start(out=idtab_flat, out_offset=AT(ap=dest_i[:, u, c:c + 1], axis=0),
                                                in_=ids_now[:, u, c:c + 1], in_offset=None).then_inc(s_idst[u], 16)
                if is_step(s, 2, ROUTE_LAST):
                    halves = hrow[:, u, 0:D].bitcast(F16)
                    if is_step(s, 2, NT - 1):
                        wait(pool, s_hst[u], 16 * (k - 1))
                        pool.nop(nofuse=True)
                        wait(pool, s_h, s - 1)
                        pool.nop(nofuse=True)
                        pool.tensor_copy(halves[:, 0:D], h32[:]).then_inc(s_hhi, 1)
                    wait(pool, s_hhi, s - 1)
                    pool.nop(nofuse=True)
                    pool.tensor_tensor(halves[:, D:2 * D], h32[:], halves[:, 0:D], ALU.subtract).then_inc(s_hlo, 1)
                if is_step(s, 0, NT - 4):
                    wait(pool, s_tr[1], s + 2)
                    pool.nop(nofuse=True)
                    load_adj(s + 3, 1 - u)
                if is_step(s, 1, NT):
                    wait(pool, s_ve, s)
                    pool.nop(nofuse=True)
                    pool.tensor_tensor(rs2[:, 1 - u:2 - u], ve2[:, 1 - u:2 - u], minus_half[:, 0:1], ALU.pow).then_inc(s_pow, 1)
                    wait(pool, s_pow, s)
                    pool.nop(nofuse=True)
                    pool.tensor_scalar(nmr2[:, 1 - u:2 - u], rs2[:, 1 - u:2 - u], mv2[:, 1 - u, 0:1], -1.0, ALU.mult, ALU.mult).then_inc(s_rs, 1)
                if is_step(s, 0, NT - 2):
                    weight_norm(s, u)
                if isinstance(s, int) and s == NT:
                    weight_norm(NT - 1, 1)

            graph_steps(pool, step)

            for u in range(2):
                pool.wait_ge(s_idst[u], 32 * (NT // 2))
            pool.wait_ge(s_blk, 1)
            pool.indirect_dma_start(out=ids[0:SLOT_TILES, :], out_offset=None, in_=idtab,
                                    in_offset=AT(ap=blk_i[0:SLOT_TILES, 0:1], axis=0)).then_inc(s_ids, 16)
            for u in range(2):
                pool.wait_ge(s_hst[u], 16 * (NT // 2))
                pool.wait_ge(s_x1st[u], 16 * (NT // 2))
            pool.wait_ge(s_table, 2)

            def gather(u, rows):
                pool.indirect_dma_start(out=xg[:, u], out_offset=None, in_=hrows,
                                        in_offset=AT(ap=rows, axis=0)).then_inc(s_xg[u], 16)

            def gather_next(t, u):
                wait(pool, s_wsel, t - 1)
                pool.nop(nofuse=True)
                wait(pool, s_xgT, t - 1)
                pool.nop(nofuse=True)
                pool.tensor_copy(src_now[:, u:u + 1], tile_src[:, bass.ds(t, 1)]).then_inc(s_src, 1)
                wait(pool, s_src, t - 1)
                pool.nop(nofuse=True)
                gather(u, src_now[:, u:u + 1])

            gather(0, tile_src[:, 0:1])
            gather(1, tile_src[:, 1:2])
            pool.wait_ge(s_table, 4)
            gather_next(2, 0)

            def scatter(t, u):
                pool.tensor_copy(dst_now[:, u:u + 1], tile_dst[:, bass.ds(t, 1)]).then_inc(s_dst, 1)
                wait(pool, s_dst, t + 1)
                pool.nop(nofuse=True)
                wait(pool, s_yg, t + 1)
                pool.nop(nofuse=True)
                wait(pool, s_add, 16 * t)
                pool.nop(nofuse=True)
                pool.indirect_dma_start(out=out, out_offset=AT(ap=dst_now[:, u:u + 1], axis=0),
                                        in_=yg[:, u], in_offset=None, bounds_check=N - 1, oob_is_err=False,
                                        compute_op=ALU.add).then_inc(s_add, 16)

            def step(t, u, k, last_of_round=False):
                if is_step(t, 0, SLOT_TILES - 4):
                    gather_next(t + 3, 1 - u)
                if is_step(t, 1, SLOT_TILES):
                    scatter(t - 1, 1 - u)

            slot_steps(pool, step, spare=3, end=SLOT_TILES + 1)
            pool.wait_ge(s_add, 16 * SLOT_TILES)

        @block.scalar
        def _(act):
            def high(g):
                act.wait_ge(s_xn, g + 1)
                act.activation(XH[:, 4 * g:4 * g + 4, 0:D], x0[:, 4 * g:4 * g + 4], ACT.Copy).then_inc(s_xh, 1)

            high(0)
            for i, (src, dst) in enumerate(((bank[2], selfT), (bank[3], nbT))):
                act.wait_ge(s_setT, i + 1)
                act.activation(dst, src[:].rearrange("p (k d) -> p k d", k=KD), ACT.Copy).then_inc(s_setTc, 1)
            for g in range(1, 4):
                high(g)
            for i, (src, dst) in enumerate(((bank[4], ws_prod), (bank[5], wn_prod))):
                act.wait_ge(s_setP, i + 1)
                act.activation(dst[:], src[:].rearrange("p (k d) -> p k d", k=KD), ACT.Copy).then_inc(s_setPc, 1)

            def weight_norm(s, u, k):
                junk, _ = wsplit(u, bass.ds(k, 1))
                wait(act, s_w[u], 16 * (k + 1))
                wait(act, s_frc, s - 1)
                act.activation(junk, stage_w(u), ACT.Square, accum_out=ssq[:, u:u + 1]).then_inc(s_sq, 1)
            def weight_high(s, u, k):
                hi, _ = wsplit(u, bass.ds(k, 1))
                wait(act, s_scale, s + 1)
                act.activation(hi, stage_w(u), ACT.Copy, scale=w_scale[:, bass.ds(s, 1)].bitcast(F32)).then_inc(s_whi, 1)

            def step(s, u, k):
                if is_step(s, 1, NT):
                    wait(act, s_pre, s)
                    wait(act, s_rdeg, s)
                    wait(act, s_prec, s - 1)
                    act.activation(mean_nb[:], pre_ps[:, 0:D], ACT.Copy, scale=rdeg[:, 1 - u:2 - u]).then_inc(s_nb, 1)
                if is_step(s, 2, ROUTE_LAST):
                    wait(act, s_ht, s - 1)
                    wait(act, s_lg, s - 2)
                    act.activation(hT[:], hT_ps, ACT.Copy).then_inc(s_htc, 1)
                if isinstance(s, int) and NT <= s <= ROUTE_LAST:
                    act.wait_ge(s_hst[u], 16 * (k - 1))
                    act.wait_ge(s_h, s - 1)
                    act.activation(hrow[:, u, 0:D].bitcast(F16)[:, 0:D], h32[:], ACT.Copy).then_inc(s_hhi, 1)
                if is_step(s, 0, NT - 1):
                    wait(act, s_agg, s + 1)
                    wait(act, s_pre, s)
                    act.activation(cT[:], agg_ps[u][:].rearrange("p (k s) -> p k s", s=P), ACT.Copy).then_inc(s_ctc, 1)
                if is_step(s, 1, NT - 1):
                    weight_high(s - 1, 1 - u, k if u else k - 1)
                if isinstance(s, int) and s == NT:
                    weight_norm(NT - 1, 1, E - 1)
                if is_step(s, 2, ROUTE_LAST):
                    wait(act, s_shift, s - 1)
                    act.activation(pexp[:], lshift[:], ACT.Exp, accum_out=psum_e[:]).then_inc(s_pexp, 1)
                if is_step(s, 0, NT - 2):
                    weight_norm(s, u, k)
                if is_step(s, 1, NT):
                    wait(act, s_rs, s)
                    wait(act, s_ht, s - 1)
                    wait(act, s_hlo, s - 1)
                    act.activation(h32[:], x1[:, 1 - u], ACT.Identity, bias=nmr2[:, 1 - u:2 - u], scale=rs2[:, 1 - u:2 - u]).then_inc(s_h, 1)
                if is_step(s, 2, ROUTE_LAST):
                    wait(act, s_vdiff, s - 1)
                    act.activation(ediff[:], vdiff[:], ACT.Exp).then_inc(s_ediff, 1)

            graph_steps(act, step)
            weight_high(NT - 1, 1, E - 1)

            act.wait_ge(s_param, 1)
            act.wait_ge(s_wlo, NT)
            act.wait_ge(s_table, 1)

            def step(t, u, k, last_of_round=False):
                e = act.value_load(tile_expert[0:1, bass.ds(t, 1)], min_val=0, max_val=E - 1)
                for half in range(2):
                    wait(act, s_mm1[half], t + 1)
                    wait(act, s_hidl[half], t)
                    for c in range(4 * half, 4 * half + 4):
                        src = bank[1 + 2 * u + half][:, (c % 4) * P:(c % 4 + 1) * P]
                        ins = act.activation(act32[:, c], src, ACT.Relu, scale=scaleA[:, bass.ds(e, 1)],
                                             bias=biasA[:, bass.ds(e, 1), c:c + 1].rearrange("p a c -> p (a c)"))
                    ins.then_inc(s_act[half], 1)

            slot_steps(act, step)

        @block.vector
        def _(dve):
            def mask(s, u, half):
                wait(dve, s_tr[half], s + 1)
                dve.tensor_scalar(maskT[:, u, HJ * half:HJ * (half + 1)], mask_ps[half], 0.0, None,
                                  ALU.is_gt).then_inc(s_mask[half], 1)

            for g in range(7):
                if g < 4:
                    dve.wait_ge(s_xin[g], 16)
                    for t in range(4 * g, 4 * g + 4):
                        dve.bn_stats(ln_stat[:, t], x0[:, t]).then_inc(s_stat, 1)
                if 1 <= g < 5:
                    part = slice(4 * g - 4, 4 * g)
                    dve.wait_ge(s_stat, 4 * g)
                    for t in range(4 * g - 4, 4 * g):
                        dve.bn_aggr(ln_mv[:, t], ln_stat[:, t]).then_inc(s_aggr, 1)
                    dve.wait_ge(s_aggr, 4 * g)
                    dve.tensor_scalar(ln_ve[:, part], ln_mv[:, part, 1], EPS, None, ALU.add).then_inc(s_lnv, 1)
                if 2 <= g < 6:
                    dve.wait_ge(s_rstd, g - 1)
                    for t in range(4 * g - 8, 4 * g - 4):
                        ins = dve.tensor_scalar(x0[:, t], x0[:, t], ln_mv[:, t, 0:1], ln_rs[:, t:t + 1], ALU.subtract, ALU.mult)
                        if t % 4 < 3:
                            ins.then_inc(s_set, 1)
                    ins.then_inc(s_xn, 1)
                if g == 4:
                    mask(0, 0, 0)
                    mask(0, 0, 1)
                if g >= 3:
                    part = slice(4 * g - 12, 4 * g - 8)
                    dve.wait_ge(s_set, 3 * (g - 2))
                    dve.wait_ge(s_xn, g - 2)
                    dve.wait_ge(s_xh, g - 2)
                    dve.tensor_tensor(XL[:, part], x0[:, part], XH[:, part, 0:D], ALU.subtract).then_inc(s_xl, 1)

            PIECES = 4
            PIECE = KD * I // PIECES

            def low_part(w, u, e, i):
                hi, lo = wsplit(u, bass.ds(e, 1))
                if i == 0:
                    wait(dve, s_whi, w + 1)
                width = I if u == 0 else D
                blk, at = divmod(i * PIECE, width)
                blk = slice(blk, blk + max(1, PIECE // width))
                at = slice(at, at + min(PIECE, width))
                ins = dve.scalar_tensor_tensor(out=lo[:, blk, at], in0=stage_w(u)[:, blk, at],
                                               scalar=w_scale[:, bass.ds(w, 1)].bitcast(F32),
                                               in1=hi[:, blk, at], op0=ALU.mult, op1=ALU.subtract)
                if i == PIECES - 1:
                    ins.then_inc(s_wlo, 1)

            GATE = 11
            SLOT = 3
            LN = 2

            dve.wait_ge(s_b1T, 1)
            dve.tensor_copy(bT[:], bank[7][:, 0:NB]).then_inc(s_b1q, 1)
            dve.wait_ge(s_b1q, 1)
            for i in range(2 * KD):
                dve.tensor_scalar(bias_cols[:, i], ones_b[:], bT[:, E * KI + i:E * KI + i + 1], None, ALU.mult).then_inc(s_bcols, 1)
            dve.tensor_tensor(b1sq, bT[:, 0:E * KI], bT[:, 0:E * KI], ALU.mult).then_inc(s_b1s, 1)
            dve.wait_ge(s_b1s, 1)
            dve.tensor_reduce(b1q[:], b1sq.rearrange("p (e c) -> p e c", e=E), AX, ALU.add).then_inc(s_b1q, 1)

            def weight_scale(s, u):
                col = bass.ds(s, 1)
                wait(dve, s_fro, s + 1)
                dve.tensor_scalar(half_exp[:, col], fro_now[:, u:u + 1].bitcast(I32), 24, None, ALU.logical_shift_right).then_inc(s_scl, 1)
                dve.tensor_copy(fro[:, col], fro_now[:, u:u + 1]).then_inc(s_frc, 1)
                wait(dve, s_scl, s + 1)
                dve.tensor_scalar(w_scale[:, col], half_exp[:, col], -float(2 ** 23), float((189 + TOP_EXP) * 2 ** 23),
                                  ALU.mult, ALU.add).then_inc(s_scale, 1)

            def step(s, u, k):
                o = 1 - u
                if is_step(s, 1, NT - 1):
                    weight_scale(s - 1, o)
                if isinstance(s, int) and s == 0:
                    mask(1, 1, 0)
                    mask(1, 1, 1)
                    dve.wait_ge(s_setP, 3)
                    dve.tensor_tensor(bias[:], bank[6][:, 0:D], bias[:], ALU.add).then_inc(s_bias, 1)
                low = (s - 1, o, k if u else k - 1) if is_step(s, 1, NT - 1) else None
                pieces = 0

                def low_pieces(n):
                    nonlocal pieces
                    if isinstance(s, int) and s == NT - 1:
                        n = 1 - pieces
                    for i in range(pieces, min(pieces + n, PIECES) if low else 0):
                        low_part(*low, i)
                        pieces = i + 1

                finishes, counts = is_step(s, 1, NT), is_step(s, 0, NT - 1)
                routes, slots = is_step(s, 2, ROUTE_LAST), is_step(s, 3, SLOT_LAST)
                c, f = s - 1, (s - 1) * LN
                r, g = s - 2, (s - 2) * GATE
                if finishes:
                    wait(dve, s_nb, c + 1)
                    dve.tensor_tensor(pre[:], mean_nb[:], pre_ps[:, D:2 * D], ALU.add).then_inc(s_prec, 1)
                if finishes:
                    wait(dve, s_prec, c + 1)
                    wait(dve, s_x[o], 16 * (k + u))
                    dve.scalar_tensor_tensor(out=x1[:, o], in0=pre[:], scalar=0.0, in1=x1[:, o],
                                             op0=ALU.max, op1=ALU.add).then_inc(s_x1, 1)
                if finishes:
                    wait(dve, s_x1, c + 1)
                    dve.bn_stats(st2[:], x1[:, o]).then_inc(s_ln, 1)
                    wait(dve, s_ln, f + 1)
                    dve.nop(nofuse=True)
                    dve.bn_aggr(mv2[:, o], st2[:]).then_inc(s_ln, 1)
                if routes:
                    wait(dve, s_lg, r + 1)
                if slots:
                    wait(dve, s_rank, s - 2)
                    dve.tensor_tensor(place[:], rank_ps, expert_base[:], ALU.add).then_inc(s_slot, 1)
                if routes:
                    dve.tensor_tensor(lg[:], lg_ps, gb[:], ALU.add).then_inc(s_lgc, 1)
                if finishes:
                    wait(dve, s_ln, f + 2)
                    dve.tensor_scalar(ve2[:, o:o + 1], mv2[:, o, 1:2], EPS, None, ALU.add).then_inc(s_ve, 1)
                if counts:
                    wait(dve, s_agg, s + 1)
                    dve.tensor_scalar(deg[:, u:u + 1], deg_ps, 1.0, None, ALU.max).then_inc(s_deg, 1)
                if routes:
                    wait(dve, s_lgc, r + 1)
                    dve.tensor_reduce(lmax[:], lg[:], AX, ALU.max).then_inc(s_gate, 1)
                if counts:
                    wait(dve, s_deg, s + 1)
                    dve.reciprocal(rdeg[:, u:u + 1], deg[:, u:u + 1]).then_inc(s_rdeg, 1)
                if slots:
                    dve.tensor_tensor(chosen_sum[:], chosen_sum[:], chosen[:, o], ALU.add).then_inc(s_slot, 1)
                    wait(dve, s_slot, (s - 3) * SLOT + 2)
                    for c in range(2):
                        ins = dve.tensor_tensor_reduce(pjunk[:, c], place[:], pick[:, o, c], 1.0, 0.0, ALU.mult, ALU.add, dest[:, c:c + 1])
                    ins.then_inc(s_slot, 1)
                if routes:
                    wait(dve, s_gate, g + 1)
                    dve.tensor_scalar(lshift[:], lg[:], lmax[:], None, ALU.subtract).then_inc(s_shift, 1)
                if slots:
                    wait(dve, s_slot, (s - 3) * SLOT + 3)
                    wait(dve, s_idst[o], 32 * (k - 2 + u))
                    dve.tensor_copy(dest_i[:, o], dest[:]).then_inc(s_dest, 1)
                low_pieces(1)
                if routes:
                    wait(dve, s_pexp, r + 1)
                    dve.reciprocal(prec[:], psum_e[:]).then_inc(s_gate, 1)
                    low_pieces(1)
                    wait(dve, s_gate, g + 2)
                    dve.tensor_scalar(prob[:], pexp[:], prec[:], None, ALU.mult).then_inc(s_gate, 1)
                    low_pieces(1)
                    wait(dve, s_gate, g + 3)
                    dve.nop(nofuse=True)
                    dve.max(top[:], prob[:]).then_inc(s_gate, 1)
                    low_pieces(1)
                    wait(dve, s_gate, g + 4)
                    dve.tensor_tensor(vdiff[:], top[:, 1:2], top[:, 0:1], ALU.subtract).then_inc(s_vdiff, 1)
                    dve.max_index(top_i[:], top[:], prob[:]).then_inc(s_gate, 1)
                if is_step(s, 0, NT - 3):
                    mask(s + 2, u, 0)
                if routes:
                    wait(dve, s_gate, g + 5)
                    dve.tensor_copy(top_f[:], top_i[:, 0:2]).then_inc(s_gate, 1)
                if is_step(s, 0, NT - 3):
                    mask(s + 2, u, 1)
                if routes:
                    wait(dve, s_gate, g + 6)
                    for c in range(2):
                        dve.tensor_scalar(pick[:, u, c], iota_e[:], top_f[:, c:c + 1], None, ALU.is_equal).then_inc(s_gate, 1)
                    wait(dve, s_ediff, r + 1)
                    dve.tensor_scalar(eplus[:], ediff[:], 1.0, None, ALU.add).then_inc(s_gate, 1)
                    wait(dve, s_gate, g + 8)
                    dve.tensor_tensor(chosen[:, u], pick[:, u, 0], pick[:, u, 1], ALU.add).then_inc(s_chosen, 1)
                    wait(dve, s_gate, g + 9)
                    dve.reciprocal(gate0[:], eplus[:]).then_inc(s_gate, 1)
                    wait(dve, s_gate, g + 10)
                    wait(dve, s_hst[u], 16 * (k - 1))
                    meta = hrow[:, u, D:ROW]
                    dve.tensor_copy(meta[:, 0:1], gate0[:]).then_inc(s_gate, 1)
                    dve.scalar_tensor_tensor(out=meta[:, 1:2], in0=ediff[:], scalar=-1.0, in1=gate0[:],
                                             op0=ALU.add, op1=ALU.mult).then_inc(s_meta, 1)
                low_pieces(PIECES)
                if isinstance(s, int) and s == NT:
                    low_part(NT - 2, 0, E - 1, 1)
                if isinstance(s, int) and s == SLOT_LAST:
                    weight_scale(NT - 1, 1)

            graph_steps(dve, step)

            dve.wait_ge(s_cnt, 1)
            n = 0

            def link(*group):
                nonlocal n
                for ins in group:
                    ins.then_inc(s_tab, 1)
                    n += 1
                dve.wait_ge(s_tab, n)

            link(dve.tensor_copy(cnt[:], cnt_ps))
            link(dve.tensor_scalar(cnt_i[:], cnt[:], float(P - 1), None, ALU.add))
            link(dve.tensor_scalar(tiles_i[:], cnt_i[:], 7, None, ALU.logical_shift_right))
            link(dve.tensor_copy(ntile[:], tiles_i[:]))
            src = ntile[:]
            for i, d in enumerate((1, 2, 4)):
                link(dve.tensor_copy(pfx[:, i, 0:d], src[:, 0:d]),
                     dve.tensor_tensor(pfx[:, i, d:E], src[:, d:E], src[:, 0:E - d], ALU.add))
                src = pfx[:, i]
            link(dve.tensor_tensor(start_t[:], src, ntile[:], ALU.subtract),
                 dve.tensor_scalar(past[:], src, iota_p[:], None, ALU.is_le))
            link(dve.scalar_tensor_tensor(out=owns[:], in0=start_t[:], scalar=iota_p[:], in1=past[:], op0=ALU.is_le, op1=ALU.subtract),
                 dve.tensor_scalar(local[:], start_t[:], iota_p[:], -1.0, ALU.subtract, ALU.mult))
            link(dve.tensor_tensor(blk[:], local[:], expert_blk[:], ALU.add),
                 dve.scalar_tensor_tensor(out=left[:], in0=local[:], scalar=-float(P), in1=cnt[:], op0=ALU.mult, op1=ALU.add))
            link(*[dve.tensor_tensor_reduce(tjunk[:, i], t[:], owns[:], 1.0, 0.0, ALU.mult, ALU.add, tcol[:, i:i + 1])
                   for i, t in enumerate((blk, left, iota_e))])
            dve.tensor_copy(blk_i[:], tcol[:, 0:1]).then_inc(s_blk, 1)

            dve.wait_ge(s_b1f, 1)
            m = 0

            def plink(ins):
                nonlocal m
                ins.then_inc(s_prm, 1)
                m += 1
                dve.wait_ge(s_prm, m)

            step_bits = float(2 ** 23)
            by_tensor = "p (e u) -> p e u"
            plink(dve.tensor_scalar(w_inv[:], half_exp[:], step_bits, float((65 - TOP_EXP) * 2 ** 23), ALU.mult, ALU.add))
            plink(dve.tensor_scalar(hq[:], b1fro[:], 2.0, None, ALU.mult))
            plink(dve.scalar_tensor_tensor(out=hq[:], in0=fro[:].rearrange(by_tensor, u=2)[:, :, 0], scalar=2.0 * D, in1=hq[:],
                                           op0=ALU.mult, op1=ALU.add))
            R = SLOT_TILES
            dve.wait_ge(s_tabT, 1)
            dve.tensor_copy(tile_expert[:], bank[3][0:1, 0:R]).then_inc(s_table, 1)
            plink(dve.tensor_scalar(h_half[:], hq[:].bitcast(I32), 24, None, ALU.logical_shift_right))
            plink(dve.tensor_scalar(h_scale[:], h_half[:], -step_bits, float((189 + TOP_EXP) * 2 ** 23), ALU.mult, ALU.add))
            plink(dve.tensor_scalar(h_inv[:], h_half[:], step_bits, float((65 - TOP_EXP) * 2 ** 23), ALU.mult, ALU.add))
            inv = w_inv[:].bitcast(F32).rearrange(by_tensor, u=2)
            plink(dve.tensor_tensor(scaleA[:], h_scale[:].bitcast(F32), inv[:, :, 0], ALU.mult))
            plink(dve.tensor_tensor(scaleY[:], h_inv[:].bitcast(F32), inv[:, :, 1], ALU.mult))
            hs = h_scale[:].bitcast(F32)
            dve.tensor_tensor(biasA[:], b1T, hs.unsqueeze(2).to_broadcast([P, E, KI]), ALU.mult).then_inc(s_param, 1)

            link(dve.tensor_scalar(beyond[0:R, :], iota_f[0:R, :], tcol[0:R, 1:2], 2.0 * N, ALU.is_ge, ALU.mult))
            for i in range(2, PIECES):
                low_part(NT - 2, 0, E - 1, i)
            dve.wait_ge(s_ids, 16)
            dve.tensor_scalar(tok_i[0:R, 0], ids[0:R, :], 1, None, ALU.logical_shift_right).then_inc(s_tok, 1)
            dve.tensor_scalar(tok_i[0:R, 1], ids[0:R, :], 1, None, ALU.bitwise_and).then_inc(s_tok, 1)
            dve.wait_ge(s_tok, 1)
            dve.tensor_copy(tok_f[0:R, 0], tok_i[0:R, 0]).then_inc(s_tokf, 1)
            dve.wait_ge(s_tok, 2)
            dve.tensor_copy(tok_f[0:R, 2], tok_i[0:R, 1]).then_inc(s_tokf, 1)
            dve.wait_ge(s_tokf, 1)
            dve.tensor_tensor(tok_f[0:R, 1], tok_f[0:R, 0], beyond[0:R, :], ALU.add).then_inc(s_tokf, 1)
            dve.wait_ge(s_tabT, 2)
            dve.tensor_copy(tile_src[:], bank[2][:, 0:R]).then_inc(s_table, 1)
            dve.wait_ge(s_tabT, 3)
            dve.tensor_copy(tile_dst[:], bank[4][:, 64:64 + R]).then_inc(s_table, 1)
            dve.tensor_copy(tile_choice[:], bank[4][:, 128:128 + R]).then_inc(s_table, 1)
            dve.wait_ge(s_table, 4)
            for i in range(PIECES):
                low_part(NT - 1, 1, E - 1, i)
            dve.wait_ge(s_b2, 16)

            def rows_turned(t, u):
                wait(dve, s_xgT, t + 1)
                dve.tensor_copy(xgT[:, u], bank[0][:, 0:2 * P].bitcast(F16).rearrange("p (j s) -> p j s", s=P)).then_inc(s_xgc, 1)

            def gate_values(t, u):
                meta = xg[:, u, D:ROW]
                dve.scalar_tensor_tensor(out=gate[:, bass.ds(t, 1)], in0=meta[:, 1:2], scalar=tile_choice[:, bass.ds(t, 1)],
                                         in1=meta[:, 0:1], op0=ALU.mult, op1=ALU.add).then_inc(s_wsel, 1)

            def rows_out(t, u, next_rows=None):
                e = dve.value_load(tile_expert[0:1, bass.ds(t, 1)], min_val=0, max_val=E - 1)
                wait(dve, s_mm2, t + 1)
                wait(dve, s_yg, t)
                dve.scalar_tensor_tensor(out=y32, in0=bank[5 + u][:, D:2 * D], scalar=scaleY[:, bass.ds(e, 1)],
                                         in1=b2_all[:, bass.ds(e, 1)].rearrange("p a d -> p (a d)"),
                                         op0=ALU.mult, op1=ALU.add).then_inc(s_ylo, 1)
                if next_rows:
                    rows_turned(*next_rows)
                wait(dve, s_ylo, t + 1)
                dve.scalar_tensor_tensor(out=y32, in0=bank[5 + u][:, 0:D], scalar=scaleY[:, bass.ds(e, 1)],
                                         in1=y32, op0=ALU.mult, op1=ALU.add).then_inc(s_y32, 1)
                if next_rows:
                    gate_values(*next_rows)
                wait(dve, s_y32, t + 1)
                wait(dve, s_wsel, t + 1)
                if not isinstance(t, int) or t >= 2:
                    wait(dve, s_add, (t - 1) * 16)
                dve.tensor_scalar(yg[:, u], y32, gate[:, bass.ds(t, 1)], None, ALU.mult).then_inc(s_yg, 1)

            for t in range(2):
                rows_turned(t, t)
                gate_values(t, t)

            def step(t, u, k, last_of_round=False):
                last = isinstance(t, int) and t == SLOT_TILES - 1
                for half in range(2):
                    if last and half == 1:
                        rows_out(t - 1, 1 - u)
                    part = slice(4 * half, 4 * half + 4)
                    wait(dve, s_act[half], t + 1)
                    dve.tensor_copy(hid_h[:, u, part], act32[:, part]).then_inc(s_hidh[half], 1)
                    wait(dve, s_hidh[half], t + 1)
                    dve.tensor_tensor(hid_l[:, u, part], act32[:, part], hid_h[:, u, part], ALU.subtract).then_inc(s_hidl[half], 1)
                if last:
                    return
                if not isinstance(t, int) or t >= 1:
                    rows_out(t - 1, 1 - u, (t + 2, u) if is_step(t, 0, SLOT_TILES - 3) else None)
                else:
                    rows_turned(t + 2, u)
                    gate_values(t + 2, u)

            slot_steps(dve, step, spare=2)
            rows_out(SLOT_TILES - 1, 0)

        @block.tensor
        def _(pe):
            def transpose_rows(s, u, k):
                wait(pe, s_adj[u], 16 * (k + 1))
                for half in range(2):
                    wait(pe, s_mask[half], s)
                    for j in range(HJ):
                        at = (half * HJ + j) * P
                        ins = pe.transpose(mask_ps[half][:, j], adj_rows[:, u, at:at + P], ident_b[:])
                    ins.then_inc(s_tr[half], 1)

            def aggregate(s, u, half):
                for j in range(HJ * half, HJ * (half + 1)):
                    if isinstance(s, int) and s == 0 and j % 4 == 0:
                        pe.wait_ge(s_xl, j // 4 + 1)
                    for kd in range(KD):
                        cols = slice(kd * P, (kd + 1) * P)
                        pe.matmul(agg_ps[u][:, cols], XH[:, j, cols], maskT[:, u, j], start=(j == 0 and kd == 0), stop=False)
                        pe.matmul(agg_ps[u][:, cols], XL[:, j, cols], maskT[:, u, j], start=False, stop=(j == NT - 1 and kd == KD - 1))

            pe.wait_ge(s_const, 14)
            pe.wait_ge(s_wself, 32)
            for src, dst in ((raw_self, bank[2]), (raw_nb, bank[3])):
                for kb in range(KD):
                    for ka in range(KD):
                        at = kb * D + ka * P
                        ins = pe.transpose(dst[:, at:at + P], src[:, ka, kb * P:(kb + 1) * P], ident_f[:])
                ins.then_inc(s_setT, 1)
            transpose_rows(0, 0, 0)
            pe.wait_ge(s_wcomb, 16)
            for i, (src, dst) in enumerate(((selfT, bank[4]), (nbT, bank[5]))):
                pe.wait_ge(s_setTc, i + 1)
                for ka in range(KD):
                    for kb in range(KD):
                        ins = pe.matmul(dst[:, ka * D:(ka + 1) * D], src[:, kb, ka * P:(ka + 1) * P], raw_comb[:, i * KD + kb],
                                        start=(kb == 0), stop=(kb == KD - 1))
                ins.then_inc(s_setP, 1)
                if i == 0:
                    pe.wait_ge(s_small, 96)
                    pe.transpose(bank[7][:, 0:NB], b_rows, ident_f[0:NB, 0:NB]).then_inc(s_b1T, 1)

            def bias_product():
                pe.wait_ge(s_bcols, 2 * KD)
                for i in range(2 * KD):
                    ins = pe.matmul(bank[6][:, 0:D], bias_cols[:, i], raw_comb[:, i], start=(i == 0), stop=(i == 2 * KD - 1))
                ins.then_inc(s_setP, 1)
                pe.wait_ge(s_setPc, 2)
                pe.wait_ge(s_bias, 1)
                pe.wait_ge(s_b1q, 1)

            def step(s, u, k):
                if is_step(s, 0, NT - 1):
                    wait(pe, s_mask[0], s + 1)
                    wait(pe, s_ctc, s - 1)
                    aggregate(s, u, 0)
                if is_step(s, 0, NT - 2):
                    transpose_rows(s + 1, 1 - u, k + u)
                if is_step(s, 0, NT - 1):
                    wait(pe, s_mask[1], s + 1)
                    aggregate(s, u, 1)
                if is_step(s, 1, NT):
                    wait(pe, s_ctc, s)
                    wait(pe, s_prec, s - 1)
                    for kd in range(KD):
                        pe.matmul(pre_ps[:, 0:D], cT[:, kd], wn_prod[:, kd], start=(kd == 0), stop=(kd == KD - 1))
                    for kd in range(KD):
                        pe.matmul(pre_ps[:, D:2 * D], cT[:, KD + kd], ws_prod[:, kd], start=(kd == 0), stop=False)
                    pe.matmul(pre_ps[:, D:2 * D], ident_f[:], bias[:], start=False, stop=True).then_inc(s_pre, 1)
                if is_step(s, 2, ROUTE_LAST):
                    wait(pe, s_h, s - 1)
                    wait(pe, s_htc, s - 2)
                    for kd in range(KD):
                        ins = pe.transpose(hT_ps[:, kd], h32[:, kd * P:(kd + 1) * P], ident_f[:])
                    ins.then_inc(s_ht, 1)
                if is_step(s, 0, NT - 1):
                    for kd in range(KD):
                        cols = slice(kd * P, (kd + 1) * P)
                        dst = agg_ps[u][:, D + kd * P:D + (kd + 1) * P]
                        pe.matmul(dst, XH[:, bass.ds(s, 1), cols].rearrange("p a d -> p (a d)"), ident_h[:], start=True, stop=False)
                        ins = pe.matmul(dst, XL[:, bass.ds(s, 1), cols].rearrange("p a d -> p (a d)"), ident_h[:], start=False, stop=True)
                    if isinstance(s, int) and s == 0:
                        pe.wait_ge(s_setPc, 1)
                    wait(pe, s_rdeg, s)
                    for j in range(NT):
                        ins = pe.matmul(deg_ps, maskT[:, u, j], XH[:, j, D:D + 1], start=(j == 0), stop=(j == NT - 1))
                    ins.then_inc(s_agg, 1)
                if isinstance(s, int) and s == 0:
                    bias_product()
                if is_step(s, 3, SLOT_LAST):
                    wait(pe, s_chosen, s - 2)
                    wait(pe, s_dest, s - 3)
                    wait(pe, s_lgc, s - 2)
                    pe.matmul(rank_ps, before[:], chosen[:, 1 - u], start=True, stop=False)
                    pe.matmul(rank_ps, ones_b[:], chosen_sum[:], start=False, stop=True).then_inc(s_rank, 1)
                if is_step(s, 2, ROUTE_LAST):
                    wait(pe, s_htc, s - 1)
                    wait(pe, s_lgc, s - 2)
                    for kd in range(KD):
                        ins = pe.matmul(lg_ps, hT[:, kd], gw[:, kd], start=(kd == 0), stop=(kd == KD - 1))
                    ins.then_inc(s_lg, 1)

            graph_steps(pe, step)

            pe.wait_ge(s_dest, NT)
            pe.matmul(cnt_ps, ones_b[:], chosen_sum[:], start=True, stop=True).then_inc(s_cnt, 1)
            R = SLOT_TILES
            pe.wait_ge(s_blk, 1)
            pe.transpose(bank[3][0:1, 0:R], tcol[0:R, 2:3], ident_f[0:R, 0:R]).then_inc(s_tabT, 1)
            pe.wait_ge(s_tokf, 1)
            pe.transpose(bank[2][:, 0:R], tok_f[0:R, 0], ident_f[0:R, 0:R]).then_inc(s_tabT, 1)
            pe.wait_ge(s_tokf, 3)
            pe.transpose(bank[4][:, 64:64 + R], tok_f[0:R, 1], ident_f[0:R, 0:R])
            pe.transpose(bank[4][:, 128:128 + R], tok_f[0:R, 2], ident_f[0:R, 0:R]).then_inc(s_tabT, 1)

            def turn_rows(t, u, k):
                wait(pe, s_xg[u], 16 * (k + 1))
                for j in range(4):
                    ins = pe.transpose(bank[0][:, 64 * j:64 * (j + 1)].bitcast(F16), xg[:, u, j * 64:(j + 1) * 64].bitcast(F16), ident_h[:])
                ins.then_inc(s_xgT, 1)

            def expert_of(t):
                return pe.value_load(tile_expert[0:1, bass.ds(t, 1)], min_val=0, max_val=E - 1)

            def up(e, t, u, c):
                if c == 0:
                    wait(pe, s_xgc, t + 1)
                dst = bank[1 + 2 * u + c // 4][:, (c % 4) * P:(c % 4 + 1) * P]
                for kd in range(KD):
                    cols = slice(c * P, (c + 1) * P)
                    hi = w1h_now[:, u, kd, cols]
                    lo = W1L[:, bass.ds(e, 1), kd, cols].rearrange("p a i -> p (a i)")
                    pe.matmul(dst, hi, xgT[:, u, kd], start=(kd == 0), stop=False)
                    pe.matmul(dst, hi, xgT[:, u, KD + kd], start=False, stop=False)
                    ins = pe.matmul(dst, lo, xgT[:, u, kd], start=False, stop=(kd == KD - 1))
                if c % 4 == 3:
                    ins.then_inc(s_mm1[c // 4], 1)

            def down(e, t, u, c):
                if c % 4 == 0:
                    wait(pe, s_hidl[c // 4], t + 1)
                both = W2S[:, bass.ds(e, 1), c].rearrange("p a d -> p (a d)")
                hi = W2S[:, bass.ds(e, 1), c, 0:D].rearrange("p a d -> p (a d)")
                pe.matmul(bank[5 + u][:], hid_h[:, u, c], both, start=(c == 0), stop=False)
                ins = pe.matmul(bank[5 + u][:, 0:D], hid_l[:, u, c], hi, start=False, stop=(c == KI - 1))
                if c == KI - 1:
                    ins.then_inc(s_mm2, 1)

            pe.wait_ge(s_table, 1)
            turn_rows(0, 0, 0)
            pe.wait_ge(s_wlo, NT)
            pe.wait_ge(s_wnow[0], 16)

            e_last = e_next = None

            def new_round():
                nonlocal e_last, e_next
                e_last = e_next = None

            def step(t, u, k, last_of_round=False):
                nonlocal e_last, e_next
                e_now = expert_of(t) if e_next is None else e_next
                if e_last is None and is_step(t, 1, SLOT_TILES):
                    e_last = expert_of(t - 1)
                for c in range(KI):
                    if c == KI - 1 and is_step(t, 0, SLOT_TILES - 2):
                        wait(pe, s_wnow[1 - u], 16 * (k + u + 1))
                    up(e_now, t, u, c)
                    if is_step(t, 1, SLOT_TILES):
                        down(e_last, t - 1, 1 - u, c)
                    if c == 3 and is_step(t, 0, SLOT_TILES - 2):
                        turn_rows(t + 1, 1 - u, k + u)
                    if c == 5:
                        e_next = expert_of(t + 1) if is_step(t, 0, SLOT_TILES - 2) and not last_of_round else None
                e_last = e_now

            slot_steps(pe, step, new_round, per_round=6, spare=1)
            for c in range(KI):
                down(e_last, SLOT_TILES - 1, 0, c)


_INS = ['x', 'adj', 'L0_gnn_W_self', 'L0_gnn_b_self', 'L0_gnn_W_nb', 'L0_gnn_b_nb', 'L0_gnn_W_comb', 'L0_gnn_b_comb',
        'L0_ffn_gate_w', 'L0_ffn_gate_b', 'L0_ffn_w1', 'L0_ffn_b1', 'L0_ffn_w2', 'L0_ffn_b2']
_OUTS = [((2048, 256), 'float32')]


def kernel(**inputs):
    import numpy as _np
    import concourse.bacc as _bacc
    from concourse import mybir as _mybir
    from concourse.bass_utils import run_bass_kernel_spmd as _run

    nc = _bacc.Bacc("TRN2", target_bir_lowering=False, num_devices=1)
    arrays, args = {}, []
    for name in _INS:
        a = _np.ascontiguousarray(inputs[name])
        arrays[f"in_{name}_dram"] = a
        args.append(nc.dram_tensor(f"in_{name}_dram", a.shape, _mybir.dt.from_np(a.dtype), kind="ExternalInput").ap())
    for i, (shape, dtype) in enumerate(_OUTS):
        dt = _mybir.dt.from_np(_np.dtype(dtype))
        args.append(nc.dram_tensor(f"out_{i}_dram", shape, dt, kind="ExternalOutput").ap())
    gnn_moe_kernel(nc, *args)
    r = _run(nc, [arrays], core_ids=[0])
    got = tuple(r.results[0][f"out_{i}_dram"] for i in range(len(_OUTS)))
    return got[0]
```
